# Optimizing a Trainium2 kernel written in Bass

```python
import numpy as np
import jax
import jax.numpy as jnp

def _softmax(x, axis=-1):
    return jax.nn.softmax(x, axis=axis)

def _gelu(x):
    return jax.nn.gelu(x, approximate=True)

def _silu(x):
    return jax.nn.silu(x)

def _sigmoid(x):
    return jax.nn.sigmoid(x)

def _layernorm(x, axis=-1, eps=1e-05):
    m = jnp.mean(x, axis=axis, keepdims=True)
    v = jnp.var(x, axis=axis, keepdims=True)
    return (x - m) / jnp.sqrt(v + eps)

def _scatter_add(tgt, idx, src, axis=0):
    return tgt.at[idx].add(src)

def _segment_sum(src, seg, n):
    return jax.ops.segment_sum(src, seg, n)
kernel_name = 'mk_adaln_d2_jaxref_r8_3ee3b4'

def setup_inputs(seed: int=0):
    np.random.seed(seed)
    _w = jnp.asarray

    def _L0_attn_setup():
        import math
        import jax, jax.numpy as jnp
        import numpy as np
        B, N, D, H = (8, 128, 256, 16)
        d = D // H
        key = jax.random.key(seed)
        ks = jax.random.split(key, 4)
        scale = 1.0 / math.sqrt(D)
        x = jax.random.normal(ks[0], (B, N, D), dtype=jnp.float32)
        Wq = jax.random.normal(ks[1], (D, D), dtype=jnp.float32) * scale
        Wk = jax.random.normal(ks[2], (D, D), dtype=jnp.float32) * scale
        Wv = jax.random.normal(ks[3], (D, D), dtype=jnp.float32) * scale
        bq = jnp.zeros((D,), dtype=jnp.float32)
        bk = jnp.zeros((D,), dtype=jnp.float32)
        bv = jnp.zeros((D,), dtype=jnp.float32)
        return {'x': x, 'Wq': Wq, 'bq': bq, 'Wk': Wk, 'bk': bk, 'Wv': Wv, 'bv': bv}
    _L0_attn_in = _L0_attn_setup()

    def _L0_ffn_setup():
        import jax, jax.numpy as jnp
        import numpy as np
        B, S, H, I, E, TOP_K, NS = (2, 256, 256, 176, 8, 2, 2)
        SI = I * NS
        INIT = 0.02
        key = jax.random.key(seed)
        ks = jax.random.split(key, 9)
        f32 = jnp.float32
        return {'hidden_states': jax.random.normal(ks[0], (B, S, H), f32), 'router_w': jax.random.normal(ks[1], (E, H), f32) * INIT, 'gate_w': jax.random.normal(ks[2], (E, H, I), f32) * INIT, 'up_w': jax.random.normal(ks[3], (E, H, I), f32) * INIT, 'down_w': jax.random.normal(ks[4], (E, I, H), f32) * INIT, 's_gate_w': jax.random.normal(ks[5], (H, SI), f32) * INIT, 's_gate_b': jnp.zeros((SI,), f32), 's_up_w': jax.random.normal(ks[6], (H, SI), f32) * INIT, 's_up_b': jnp.zeros((SI,), f32), 's_down_w': jax.random.normal(ks[7], (SI, H), f32) * INIT, 's_down_b': jnp.zeros((H,), f32)}
    _L0_ffn_in = _L0_ffn_setup()
    _L0_c = _w((lambda *s: np.random.randn(*s).astype(np.float32) * 0.05)(1, 256))
    _L0_wmod = _w((lambda *s: np.random.randn(*s).astype(np.float32) * 0.05)(256, 6 * 256) * 256 ** (-0.5))

    def _L1_attn_setup():
        import jax, jax.numpy as jnp
        import numpy as np
        import math
        D = 32
        N = 256
        B = 8
        N_PLUS_1 = 256
        key = jax.random.key(seed)
        k1, k2, k3, k4, k5 = jax.random.split(key, 5)
        scale = 1.0 / math.sqrt(D)
        return {'Z_in': jax.random.normal(k1, (B, D + 1, N), dtype=jnp.float32), 'A_l': jax.random.normal(k2, (D, D), dtype=jnp.float32) * scale, 'r_l': jax.random.normal(k3, (1,), dtype=jnp.float32), 'B_l': jax.random.normal(k4, (D, D), dtype=jnp.float32) * scale, 'C_l': jax.random.normal(k5, (D, D), dtype=jnp.float32) * scale}
    _L1_attn_in = _L1_attn_setup()

    def _L1_ffn_setup():
        import jax, jax.numpy as jnp
        import numpy as np

        def binarize_weight(w):
            alpha = jnp.mean(jnp.abs(w), axis=tuple(range(1, w.ndim)), keepdims=True)
            bw = jnp.where(w >= 0, 1.0, -1.0) * alpha
            return jax.lax.stop_gradient(bw - w) + w
        key = jax.random.key(seed)
        k1, k2, k3 = jax.random.split(key, 3)
        in_features, out_features = (256, 256)
        x = jax.random.normal(k1, (8, 256, in_features), dtype=jnp.float32)
        std = np.sqrt(2.0 / out_features).astype(np.float32)
        weight = jax.random.normal(k2, (out_features, in_features), dtype=jnp.float32) * std
        bias = jax.random.normal(k3, (out_features,), dtype=jnp.float32) * 0.01
        return {'x': x, 'weight': weight, 'bias': bias}
    _L1_ffn_in = _L1_ffn_setup()
    _L1_c = _w((lambda *s: np.random.randn(*s).astype(np.float32) * 0.05)(1, 256))
    _L1_wmod = _w((lambda *s: np.random.randn(*s).astype(np.float32) * 0.05)(256, 6 * 256) * 256 ** (-0.5))
    _d = {'L0_attn_x': _L0_attn_in['x'], 'L0_attn_Wq': _L0_attn_in['Wq'], 'L0_attn_bq': _L0_attn_in['bq'], 'L0_attn_Wk': _L0_attn_in['Wk'], 'L0_attn_bk': _L0_attn_in['bk'], 'L0_attn_Wv': _L0_attn_in['Wv'], 'L0_attn_bv': _L0_attn_in['bv'], 'L0_ffn_router_w': _L0_ffn_in['router_w'], 'L0_ffn_gate_w': _L0_ffn_in['gate_w'], 'L0_ffn_up_w': _L0_ffn_in['up_w'], 'L0_ffn_down_w': _L0_ffn_in['down_w'], 'L0_ffn_s_gate_w': _L0_ffn_in['s_gate_w'], 'L0_ffn_s_gate_b': _L0_ffn_in['s_gate_b'], 'L0_ffn_s_up_w': _L0_ffn_in['s_up_w'], 'L0_ffn_s_up_b': _L0_ffn_in['s_up_b'], 'L0_ffn_s_down_w': _L0_ffn_in['s_down_w'], 'L0_ffn_s_down_b': _L0_ffn_in['s_down_b'], 'L0_c': _L0_c, 'L0_wmod': _L0_wmod, 'L1_attn_A_l': _L1_attn_in['A_l'], 'L1_attn_r_l': _L1_attn_in['r_l'], 'L1_attn_B_l': _L1_attn_in['B_l'], 'L1_attn_C_l': _L1_attn_in['C_l'], 'L1_ffn_weight': _L1_ffn_in['weight'], 'L1_ffn_bias': _L1_ffn_in['bias'], 'L1_c': _L1_c, 'L1_wmod': _L1_wmod}
    _x0 = _d['L0_attn_x']
    _d['L0_attn_x'] = jax.random.normal(jax.random.fold_in(jax.random.key(seed), 1), (1, 2048, 256), dtype=_x0.dtype)
    del _x0
    return _d

def reference(L0_attn_x, L0_attn_Wq, L0_attn_bq, L0_attn_Wk, L0_attn_bk, L0_attn_Wv, L0_attn_bv, L0_ffn_router_w, L0_ffn_gate_w, L0_ffn_up_w, L0_ffn_down_w, L0_ffn_s_gate_w, L0_ffn_s_gate_b, L0_ffn_s_up_w, L0_ffn_s_up_b, L0_ffn_s_down_w, L0_ffn_s_down_b, L0_c, L0_wmod, L1_attn_A_l, L1_attn_r_l, L1_attn_B_l, L1_attn_C_l, L1_ffn_weight, L1_ffn_bias, L1_c, L1_wmod):

    def _L0_attn_ref(x, Wq, bq, Wk, bk, Wv, bv):
        import math
        import jax, jax.numpy as jnp
        import numpy as np
        B, N, D, H = (8, 128, 256, 16)
        d = D // H
        Bn, Nn, Dn = x.shape
        q = (x @ Wq + bq).reshape(Bn, Nn, H, d)
        k = (x @ Wk + bk).reshape(Bn, Nn, H, d)
        v = (x @ Wv + bv).reshape(Bn, Nn, H, d)
        scores = jnp.einsum('bnhd,bmhd->bnmh', q, k) / math.sqrt(d)
        att = jax.nn.softmax(scores, axis=2)
        attval = jnp.einsum('bnmh,bmhd->bnhd', att, v).reshape(Bn, Nn, Dn)
        return attval + x

    def _L0_ffn_ref(hidden_states, router_w, gate_w, up_w, down_w, s_gate_w, s_gate_b, s_up_w, s_up_b, s_down_w, s_down_b):
        import jax, jax.numpy as jnp
        import numpy as np
        B, S, H, I, E, TOP_K, NS = (2, 256, 256, 176, 8, 2, 2)
        SI = I * NS
        INIT = 0.02
        b, s, h = hidden_states.shape
        x = hidden_states.reshape(-1, h)
        T = x.shape[0]
        num_experts = router_w.shape[0]
        logits = x @ router_w.T
        probs = jax.nn.softmax(logits.astype(jnp.float32), axis=-1)
        topk_w, topk_idx = jax.lax.top_k(probs, TOP_K)
        topk_w = topk_w / jnp.sum(topk_w, axis=-1, keepdims=True)
        combine = jnp.zeros((T, num_experts), probs.dtype)
        combine = combine.at[jnp.arange(T)[:, None], topk_idx].add(topk_w)

        def expert_step(acc, ws):
            gw, uw, dw, ce = ws
            out = jax.nn.silu(x @ gw) * (x @ uw) @ dw
            return (acc + ce[:, None].astype(out.dtype) * out, None)
        moe_out, _ = jax.lax.scan(expert_step, jnp.zeros_like(x), (gate_w, up_w, down_w, combine.T))
        shared = jax.nn.silu(x @ s_gate_w + s_gate_b) * (x @ s_up_w + s_up_b) @ s_down_w + s_down_b
        return (moe_out + shared).reshape(b, s, h)

    def _L1_attn_ref(Z_in, A_l, r_l, B_l, C_l):
        import jax, jax.numpy as jnp
        import numpy as np
        import math
        D = 32
        N = 256
        B = 8
        N_PLUS_1 = 256
        X = Z_in[:, :D, :]
        Y = Z_in[:, D:, :]
        U = jnp.einsum('ij,bjn->bin', B_l, X)
        W = jnp.einsum('ij,bjn->bin', C_l, X)
        scores = jnp.einsum('bdn,bdm->bnm', U, W)
        att = jax.nn.relu(scores)
        att = att.at[:, N_PLUS_1 - 1, N_PLUS_1 - 1].set(0.0)
        X_att = jnp.einsum('bdn,bnm->bdm', X, att)
        X_out = X + jnp.einsum('ij,bjm->bim', A_l, X_att)
        Y_out = Y + r_l * jnp.einsum('bdn,bnm->bdm', Y, att)
        return jnp.concatenate([X_out, Y_out], axis=1)

    def _L1_ffn_ref(x, weight, bias):
        import jax, jax.numpy as jnp
        import numpy as np

        def binarize_weight(w):
            alpha = jnp.mean(jnp.abs(w), axis=tuple(range(1, w.ndim)), keepdims=True)
            bw = jnp.where(w >= 0, 1.0, -1.0) * alpha
            return jax.lax.stop_gradient(bw - w) + w
        bw = binarize_weight(weight)
        return jnp.einsum('bsi,oi->bso', x, bw) + bias
    x = L0_attn_x
    mod = (_silu(L0_c) @ L0_wmod).reshape(L0_c.shape[0], 6, 1, -1)
    sa, ca, ga, sb, cb, gb = (mod[:, 0], mod[:, 1], mod[:, 2], mod[:, 3], mod[:, 4], mod[:, 5])
    ga = (2 * (ga >= 0) - 1) * jnp.maximum(jnp.abs(ga), 0.25)
    gb = (2 * (gb >= 0) - 1) * jnp.maximum(jnp.abs(gb), 0.25)
    h = _layernorm(x, axis=-1) * (1 + ca) + sa
    x = x + ga * _L0_attn_ref(h, L0_attn_Wq, L0_attn_bq, L0_attn_Wk, L0_attn_bk, L0_attn_Wv, L0_attn_bv)
    h = _layernorm(x, axis=-1) * (1 + cb) + sb
    x = x + gb * _L0_ffn_ref(h, L0_ffn_router_w, L0_ffn_gate_w, L0_ffn_up_w, L0_ffn_down_w, L0_ffn_s_gate_w, L0_ffn_s_gate_b, L0_ffn_s_up_w, L0_ffn_s_up_b, L0_ffn_s_down_w, L0_ffn_s_down_b)
    mod = (_silu(L1_c) @ L1_wmod).reshape(L1_c.shape[0], 6, 1, -1)
    sa, ca, ga, sb, cb, gb = (mod[:, 0], mod[:, 1], mod[:, 2], mod[:, 3], mod[:, 4], mod[:, 5])
    ga = (2 * (ga >= 0) - 1) * jnp.maximum(jnp.abs(ga), 0.25)
    gb = (2 * (gb >= 0) - 1) * jnp.maximum(jnp.abs(gb), 0.25)
    h = _layernorm(x, axis=-1) * (1 + ca) + sa
    x = x + ga * _L1_attn_ref(h, L1_attn_A_l, L1_attn_r_l, L1_attn_B_l, L1_attn_C_l)
    h = _layernorm(x, axis=-1) * (1 + cb) + sb
    x = x + gb * _L1_ffn_ref(h, L1_ffn_weight, L1_ffn_bias)
    return x

_drawn_inputs = setup_inputs


def setup_inputs(seed=0):
    import zlib

    import numpy as np

    out = dict(_drawn_inputs(seed))
    spreads = {'L0_attn_bq': (0.0, 0.8),
     'L0_attn_bk': (0.0, 2.0),
     'L0_attn_bv': (0.0, 0.1),
     'L0_ffn_s_gate_b': (0.0, 0.8),
     'L0_ffn_s_up_b': (0.0, 0.8),
     'L0_ffn_s_down_b': (0.0, 0.431)}
    factors = {'L0_ffn_router_w': 8.0,
     'L0_ffn_gate_w': 8.0,
     'L0_ffn_up_w': 8.0,
     'L0_ffn_down_w': 8.0,
     'L0_ffn_s_gate_w': 6.185,
     'L0_ffn_s_up_w': 6.212,
     'L0_ffn_s_down_w': 6.019,
     'L1_ffn_weight': 3.994,
     'L1_ffn_bias': 200.0}
    for name, (base, spread) in spreads.items():
        noise = np.random.default_rng([zlib.crc32(name.encode()), seed]).standard_normal(out[name].shape)
        drawn = base * np.exp(spread * noise) if base else spread * noise
        out[name] = jnp.asarray(drawn.astype(out[name].dtype))
    for name, factor in factors.items():
        out[name] = (out[name] * factor).astype(out[name].dtype)
    return out
```

```python
import struct
from contextlib import ExitStack

import concourse.bass as bass
import numpy as np
from concourse import mybir

F32 = mybir.dt.float32
BF16 = mybir.dt.bfloat16
ALU = mybir.AluOpType
ACT = mybir.ActivationFunctionType
AX = mybir.AxisListType

P = 128
T, D = 2048, 256
KT = D // P
NT = T // P
CH = 512
NC = T // CH
TPC = CH // P
H, DH = 16, 16
G = 4
NG = H // G
NU = NC * NG
MT = T // P
BLK = 6
KR = BLK * DH
NM = 3
Q_PART = (0, 0, 1, 0, 2, 1)
K_PART = (0, 1, 0, 2, 0, 1)
VW = 32
E, I, SI = 8, 176, 352
IE = E * I // P
IA = E * I + SI
NI = -(-IA // P)
LAST = IA - (NI - 1) * P
DX = 32
EPS = 1e-5
LEAD = 4
MI = G * TPC


def build(nc, x_in, wq, bq, wk, bk, wv, bv, routerT, gate_w, up_w, down_w, sg_w, sg_b, su_w, su_b,
          sd_w, sd_b, c0, wmod0, AT, r_l, BT, CT, w1, b1, c1, wmod1, out):
    ctx = ExitStack()
    base = -(-nc.sbuf_base // 64) * 64
    top = [base]

    def region(nbytes):
        at = top[0]
        top[0] += -(-nbytes // 32) * 32
        assert top[0] <= nc.sbuf_usable_end, top[0]
        return at

    def at(name, shape, dt, offset):
        return nc.alloc_sbuf_tensor_at(name, shape, dt, offset=offset)

    def new(name, shape, dt=F32):
        n = int(np.prod(shape[1:])) * (2 if dt == BF16 else 4)
        return at(name, shape, dt, region(n))

    with ctx:
        x = new("x", [P, NT, D])
        hT = new("hT", [P, KT, T])
        ident = new("ident", [P, P])
        wv_sb = new("wv_sb", [P, KT, D])
        bv_row = new("bv_row", [P, D])
        rows0 = new("rows0", [P, 4, D])
        GCA, GSA, GA, GB = range(4)
        mcol = [new(f"mcol{n}", [P, 12]) for n in range(2)]
        mvs = [new(f"mv{n}", [P, NT, 2]) for n in range(4)]
        rss = [new(f"rs{n}", [P, NT]) for n in range(4)]
        bn_st = new("bn_st", [P, TPC, 6])
        std = new("std", [P, TPC])
        eps = new("eps", [P, 1])
        c_col = [new(f"c_col{n}", [P, KT]) for n in range(2)]
        c_sil = [new(f"c_sil{n}", [P, KT]) for n in range(2)]
        bq_col, bk_col = new("bq_col", [P, KT]), new("bk_col", [P, KT])
        mxp = new("mxp", [P, MI, 2])
        nmx = new("nmx", [P, MI])
        nm32, nmr = new("nm32", [MI, P]), new("nmr", [MI, P])
        nmp = new("nmp", [MI, NM, P], BF16)
        rec = new("rec", [P, TPC, G])
        rw = new("rw", [P, KT, E])
        bg, bu = new("bg", [P, NI]), new("bu", [P, NI])
        AT_sb, BT_sb, CT_sb = new("AT_sb", [DX, DX]), new("BT_sb", [DX, DX]), new("CT_sb", [DX, DX])
        r_col = new("r_col", [P, 1])

        k_reg = region(H * T * 2)
        q_reg = region(4 * G * CH * 2)
        qp_reg = region(KT * 3 * T * 2)
        p_reg = region(2 * G * CH * 4)
        e_reg = region(8192)
        v_reg = region(MT * H * VW * 4)

        kst = at("kst", [P, H, T], BF16, k_reg)
        qst = at("qst", [P, 4, G, CH], BF16, q_reg)
        xh = at("xh", [P, 2, TPC, D], F32, q_reg)
        q32 = at("q32", [P, 2, CH], F32, q_reg + 8192)
        res = at("res", [P, 2, CH], F32, q_reg + 8192 + 4096)
        qp = at("qp", [P, KT, 3, T], BF16, qp_reg)
        kp = at("kp", [P, KT, 3, T], BF16, p_reg)
        prob = at("prob", [P, 2, G, CH], F32, p_reg)
        o_sb = at("o_sb", [P, CH], F32, e_reg)
        o_tm = at("o_tm", [P, TPC, G, VW], F32, e_reg + 2048)
        att_u = at("att_u", [P, TPC, G, DH], F32, e_reg + 4096)
        xt = at("xt", [P, D], F32, e_reg + 5120)
        vp = at("vp", [P, MT, H, VW], F32, v_reg)
        wmod_sb = at("wmod_sb", [P, KT, 6 * D], F32, v_reg)
        mrow = at("mrow", [P, 6, D], F32, v_reg + 12288)
        cb = at("cb", [P, KT, P], F32, v_reg + 18432)
        wk_sb = at("wk_sb", [P, KT, D], F32, v_reg + 28672)
        wq_sb = at("wq_sb", [P, KT, D], F32, v_reg + 30720)
        wg_sb = at("wg_sb", [P, KT, IA], F32, k_reg)
        wu_sb = at("wu_sb", [P, KT, IA], F32, k_reg + 16384)
        wd_sb = at("wd_sb", [P, NI, D], F32, k_reg + 32768)
        hid = at("hid", [P, 2, CH], F32, k_reg + 49152)
        sig = at("sig", [P, 2, CH], F32, k_reg + 49152 + 4096)
        tmul = at("tmul", [P, 2, CH], F32, k_reg + 49152 + 8192)
        yt = at("yt", [P, TPC, D], F32, k_reg + 49152 + 12288)
        sel = at("sel", [E, E * I], F32, qp_reg)
        ceT = at("ceT", [E, T], F32, qp_reg + 5632)
        lg = at("lg", [P, NT, E], F32, qp_reg + 13824)
        pr = at("pr", [P, NT, E], F32, qp_reg + 13824 + 512)
        rank = at("rank", [P, NT, E], F32, qp_reg + 13824 + 1024)
        r16 = at("r16", [P, NT], F32, qp_reg + 13824 + 1536)
        r16b = at("r16b", [P, NT], F32, qp_reg + 13824 + 1600)
        tri = at("tri", [P, E, E], F32, qp_reg + 13824 + 1664)
        cmp1 = at("cmp1", [P, NT, E, E], F32, qp_reg + 16384)
        cmp2 = at("cmp2", [P, NT, E, E], F32, qp_reg + 20480)
        rows1 = at("rows1", [P, 5, D], F32, p_reg)
        RGA = 4
        gsd = at("gsd", [P, D], F32, p_reg + 5120)
        gb1 = at("gb1", [P, D], F32, p_reg + 6144)
        sdb_row = at("sdb_row", [P, D], F32, p_reg + 7168)
        b1_row = at("b1_row", [P, D], F32, p_reg + 8192)
        w1_sb = at("w1_sb", [P, KT, D], F32, p_reg + 9216)
        bw = at("bw", [P, KT, D], F32, p_reg + 11264)
        bwT = at("bwT", [P, KT, D], F32, p_reg + 13312)
        alpha = at("alpha", [P, KT], F32, p_reg + 15360)
        ux = at("ux", [DX, D], F32, v_reg + 20480)
        uu = at("uu", [DX, D], F32, v_reg + 21504)
        ww = at("ww", [DX, D], F32, v_reg + 22528)
        xa = at("xa", [DX, D], F32, v_reg + 23552)
        att = at("att", [P, KT, D], F32, v_reg + 24576)
        yt2 = at("yt2", [P, 2, D], F32, v_reg + 26624)

        ps = ctx.enter_context(nc.psum_tensor("ps", [P, 8, CH], F32))

        names = {}

        def sem(name):
            names[name] = ctx.enter_context(nc.semaphore(name))
            return names[name]

        x_in_s = [sem(f"x_loaded{c}") for c in range(NC)]
        mod_in, wqk_in, wv_in, small_in = sem("mod_in"), sem("wqk_in"), sem("wv_in"), sem("small_in")
        consts, bias0 = sem("consts"), sem("bias0")
        c_ready, cb_ready, mcol_ps, mrow_ps = sem("c_ready"), sem("cb_ready"), sem("mcol_ps"), sem("mrow_ps")
        mcol_ready, mrow_ready, rows_step = sem("mcol_ready"), sem("mrow_ready"), sem("rows_step")
        bn_s, var_s, std_s, rs_s, xh_s = sem("bn_s"), sem("var_s"), sem("std_s"), sem("rs_s"), sem("xh_s")
        tr_ps, hT_s = sem("tr_ps"), sem("hT_s")
        proj_ps, q32_s, hi_s, r_s, mid_s, split_s = (sem("proj_ps"), sem("q32_s"), sem("hi_s"), sem("r_s"),
                                                     sem("mid_s"), sem("split_s"))
        v_ps, v_s, vconst = sem("v_ps"), sem("v_s"), sem("vconst")
        kst_in = [sem(f"kst_in{g}") for g in range(3)]
        kd_out, qd_out = sem("kd_out"), sem("qd_out")
        kst_one, q_in, nm_in = sem("kst_one"), sem("q_in"), sem("nm_in")
        mx_ps, mx_read, nmx_s = sem("mx_ps"), sem("mx_read"), sem("nmx_s")
        nmT_ps, nmT_s, nm_step, nm_s = sem("nmT_ps"), sem("nmT_s"), sem("nm_step"), sem("nm_s")
        sc_ps, p_s, pv_s, o_s, oT_ps, oT_s = sem("sc_ps"), sem("p_s"), sem("pv_s"), sem("o_s"), sem("oT_ps"), sem("oT_s")
        rec_s, att_step, att_s = sem("rec_s"), sem("att_step"), sem("att_s")
        res_step, res_s = sem("res_step"), sem("res_s")
        ffw_in = [sem(f"ffw_in{n}") for n in range(3)]
        l1_in, mod1_in = sem("l1_in"), sem("mod1_in")
        lg_ps, rt, ce_ps, ceT_s, sel_s = sem("lg_ps"), sem("rt"), sem("ce_ps"), sem("ceT_s"), sem("sel_s")
        exp_s, ce_s = sem("exp_s"), sem("ce_s")
        gu_ps, sig_s, t_s, cb_ps, hid_s, hid_used = (sem("gu_ps"), sem("sig_s"), sem("t_s"), sem("cb_ps"),
                                                     sem("hid_s"), sem("hid_used"))
        y_ps, y_read, y_s, xsd_s = sem("y_ps"), sem("y_read"), sem("y_s"), sem("xsd_s")
        l1_step, ux_s, uw_ps, uw_s, s1_ps, relu_s, att_z = (sem("l1_step"), sem("ux_s"), sem("uw_ps"), sem("uw_s"),
                                                            sem("s1_ps"), sem("relu_s"), sem("att_z"))
        za_ps, za_read, za_s, xa_s, axa_ps = sem("za_ps"), sem("za_read"), sem("za_s"), sem("xa_s"), sem("axa_ps")
        bw_s, bwT_ps, bwT_s, f_ps, f_read, f_s = (sem("bw_s"), sem("bwT_ps"), sem("bwT_s"), sem("f_ps"),
                                                  sem("f_read"), sem("f_s"))
        res1_s, res1_step, xb_s, out_s, axa_s = sem("res1_s"), sem("res1_step"), sem("xb_s"), sem("out_s"), sem("axa_s")

        block = ctx.enter_context(nc.Block())
        kd = nc.dram_tensor("k_parts", (3, D, T), BF16, kind="Internal").ap()
        qd = nc.dram_tensor("q_parts", (3, D, T), BF16, kind="Internal").ap()
        x_v = x_in.rearrange("(t p) d -> p t d", p=P)
        out_v = out.rearrange("(t p) d -> p t d", p=P)

        def ln(n, c):
            return NC * n + c

        @block.sync
        def _(sp):
            for c in range(NC):
                sp.dma_start(x[:, TPC * c:TPC * (c + 1), :], x_v[:, TPC * c:TPC * (c + 1), :]).then_inc(x_in_s[c], 16)
            sp.dma_start(wk_sb[:], wk.rearrange("(k p) n -> p k n", p=P)).then_inc(wqk_in, 16)
            sp.dma_start(wq_sb[:], wq.rearrange("(k p) n -> p k n", p=P)).then_inc(wqk_in, 16)
            sp.dma_start(wv_sb[:], wv.rearrange("(k p) n -> p k n", p=P)).then_inc(wv_in, 16)
            sp.dma_start(bv_row[:], bv.unsqueeze(0).to_broadcast([P, D])).then_inc(wv_in, 16)

            def store_parts(src, dst, ft, c, sem_):
                cols = slice(CH * c, CH * (c + 1))
                sp.dma_start(dst[:, P * ft:P * (ft + 1), cols].rearrange("a p n -> p a n"),
                             src[:, ft, :, cols]).then_inc(sem_, 16)

            def load_k(g, sem_):
                for b in range(BLK):
                    sp.dma_start(kst[DH * b:DH * (b + 1), G * g:G * (g + 1), :],
                                 kd[K_PART[b]].rearrange("(h d) n -> d h n", d=DH)[:, G * g:G * (g + 1), :]
                                 ).then_inc(sem_, 16)

            def load_q(g, c):
                for b in range(BLK):
                    sp.dma_start(qst[DH * b:DH * (b + 1), g, :, :],
                                 qd[Q_PART[b]].rearrange("(h d) n -> d h n", d=DH)[:, G * g:G * (g + 1), bass.ts(c, CH)]
                                 ).then_inc(q_in, 16)

            def store_max(slot):
                for m in range(NM):
                    sp.dma_start(qst[KR + m:KR + m + 1, slot, :, :].rearrange("p k (j n) -> p (k j) n", j=TPC),
                                 nmp[:, m, :]).then_inc(nm_in, 16)

            for c in range(NC):
                for ft in range(KT):
                    sp.wait_ge(split_s, KT * c + ft + 1)
                    store_parts(kp, kd, ft, c, kd_out)
            sp.wait_ge(kd_out, 16 * KT * NC)
            load_k(0, kst_in[0])
            for c in range(NC):
                for ft in range(KT):
                    sp.wait_ge(split_s, KT * NC + KT * c + ft + 1)
                    store_parts(qp, qd, ft, c, qd_out)
                if c == 0:
                    sp.wait_ge(qd_out, 16 * KT)
                    load_q(0, 0)
                    load_k(1, kst_in[1])
                    sp.wait_ge(q_in, 16 * BLK)
                    load_q(1, 0)
                    sp.wait_ge(q_in, 16 * BLK * 2)
            load_k(2, kst_in[2])
            load_k(3, kst_in[2])
            sp.wait_ge(qd_out, 16 * KT * NC)
            sp.wait_ge(nm_s, 1)
            store_max(0)
            sp.wait_ge(nm_in, 16 * NM)
            for v in range(2, G):
                load_q(v, 0)
                sp.wait_ge(q_in, 16 * BLK * (v + 1))
                sp.wait_ge(nm_s, v)
                store_max(v - 1)
                sp.wait_ge(nm_in, 16 * NM * v)
            for v in range(G, NU):
                c, g = v // NG, v % NG
                sp.wait_ge(sc_ps, G * MT * (v - NG + 1))
                load_q(g, c)
                sp.wait_ge(q_in, 16 * BLK * (v + 1))
                sp.wait_ge(nm_s, v)
                store_max((v - 1) % NG)
                sp.wait_ge(nm_in, 16 * NM * v)
            sp.wait_ge(nm_s, NU)
            store_max(NG - 1)
            sp.wait_ge(sc_ps, G * MT * (NU - 3))
            sp.dma_start(wg_sb[:, :, 0:E * I].rearrange("p k (e i) -> p k e i", e=E)[:, 0],
                         gate_w.rearrange("e (k p) i -> k p e i", p=P)[0]).then_inc(ffw_in[0], 16)
            sp.dma_start(wg_sb[:, :, 0:E * I].rearrange("p k (e i) -> p k e i", e=E)[:, 1],
                         gate_w.rearrange("e (k p) i -> k p e i", p=P)[1]).then_inc(ffw_in[0], 16)
            sp.dma_start(wg_sb[:, :, E * I:IA], sg_w.rearrange("(k p) i -> p k i", p=P)).then_inc(ffw_in[0], 16)
            sp.wait_ge(sc_ps, G * MT * (NU - 2))
            sp.dma_start(wu_sb[:, :, 0:E * I].rearrange("p k (e i) -> p k e i", e=E)[:, 0],
                         up_w.rearrange("e (k p) i -> k p e i", p=P)[0]).then_inc(ffw_in[1], 16)
            sp.dma_start(wu_sb[:, :, 0:E * I].rearrange("p k (e i) -> p k e i", e=E)[:, 1],
                         up_w.rearrange("e (k p) i -> k p e i", p=P)[1]).then_inc(ffw_in[1], 16)
            sp.dma_start(wu_sb[:, :, E * I:IA], su_w.rearrange("(k p) i -> p k i", p=P)).then_inc(ffw_in[1], 16)
            sp.wait_ge(sc_ps, G * MT * (NU - 1))
            sp.dma_start(wd_sb[:, 0:IE, :], down_w.rearrange("e i d -> (e i) d").rearrange("(t p) d -> p t d", p=P)
                         ).then_inc(ffw_in[2], 16)
            sp.dma_start(wd_sb[:, IE:NI - 1, :], sd_w[0:(NI - 1 - IE) * P, :].rearrange("(t p) d -> p t d", p=P)
                         ).then_inc(ffw_in[2], 16)
            sp.dma_start(wd_sb[0:LAST, NI - 1, :], sd_w[(NI - 1 - IE) * P:SI, :]).then_inc(ffw_in[2], 16)
            sp.wait_ge(pv_s, MT * NU)
            sp.dma_start(wmod_sb[:], wmod1.rearrange("(k p) n -> p k n", p=P)).then_inc(mod1_in, 16)
            sp.wait_ge(att_s, NU)
            sp.dma_start(sdb_row[:], sd_b.unsqueeze(0).to_broadcast([P, D])).then_inc(l1_in, 16)
            sp.dma_start(b1_row[:], b1.unsqueeze(0).to_broadcast([P, D])).then_inc(l1_in, 16)
            sp.dma_start(w1_sb[:], w1.rearrange("(k p) n -> p k n", p=P)).then_inc(l1_in, 16)
            for c in range(NC):
                sp.wait_ge(f_s, TPC * (c + 1))
                sp.dma_start(out_v[:, TPC * c:TPC * (c + 1), :], x[:, TPC * c:TPC * (c + 1), :]).then_inc(out_s, 16)
            sp.wait_ge(out_s, 16 * NC)

        @block.tensor
        def _(pe):
            def modulation(n):
                for j in range(12):
                    for k in range(KT):
                        last = nc.tensor.matmul(ps[:, 7, j:j + 1], wmod_sb[:, k, P * j:P * (j + 1)],
                                                c_sil[n][:, k:k + 1], start=k == 0, stop=k == KT - 1)
                last.then_inc(mcol_ps, 1)
                for j in range(3):
                    for k in range(KT):
                        last = nc.tensor.matmul(ps[:, 4 + j, :], cb[:, k, :], wmod_sb[:, k, CH * j:CH * (j + 1)],
                                                start=k == 0, stop=k == KT - 1)
                last.then_inc(mrow_ps, 1)

            def transposes(n, c):
                q = ln(n, c)
                pe.wait_ge(xh_s, TPC * (q + 1))
                pe.wait_ge(hT_s, KT * q)
                for ft in range(KT):
                    for j in range(TPC):
                        last = nc.tensor.transpose(ps[:, ft, P * j:P * (j + 1)],
                                                   xh[:, q % 2, j, P * ft:P * (ft + 1)], ident[:])
                    last.then_inc(tr_ps, 1)

            def project(i, w, c, ft):
                pe.wait_ge(hT_s, KT * (c + 1))
                if i >= 2:
                    pe.wait_ge(q32_s, i - 1)
                for k in range(KT):
                    last = nc.tensor.matmul(ps[:, 2 + i % 2, :], w[:, k, P * ft:P * (ft + 1)],
                                            hT[:, k, CH * c:CH * (c + 1)], start=k == 0, stop=k == KT - 1)
                last.then_inc(proj_ps, 1)

            pe.wait_ge(mod_in, 32)
            pe.wait_ge(c_ready, 1)
            pe.wait_ge(cb_ready, 1)
            modulation(0)
            pe.wait_ge(consts, 1)
            transposes(0, 0)
            pe.wait_ge(wqk_in, 32)
            for c in range(1, NC):
                transposes(0, c)
                for ft in range(KT):
                    project(KT * (c - 1) + ft, wk_sb, c - 1, ft)
            for ft in range(KT):
                project(KT * (NC - 1) + ft, wk_sb, NC - 1, ft)
            for c in range(NC):
                for ft in range(KT):
                    project(KT * NC + KT * c + ft, wq_sb, c, ft)
            pe.wait_ge(wv_in, 32)
            for i in range(MT // 2):
                if i < 2:
                    pe.wait_ge(mrow_ready, 1)
                else:
                    pe.wait_ge(v_s, i - 1)
                for j in range(2):
                    for k in range(KT):
                        last = nc.tensor.matmul(ps[:, 4 + i % 2, D * j:D * (j + 1)],
                                                hT[:, k, P * (2 * i + j):P * (2 * i + j + 1)], wv_sb[:, k, :],
                                                start=k == 0, stop=k == KT - 1)
                last.then_inc(v_ps, 1)

            def maxima(g, i, p, n):
                if not isinstance(n, int) or n >= 2:
                    pe.wait_ge(mx_read, n - 1)
                hd, j = i // TPC, i % TPC
                for m in range(2):
                    col = CH * (2 * p + m)
                    last = nc.tensor.matmul(ps[:, 2 * p + m, :], qst[0:KR, g, hd, P * j:P * (j + 1)],
                                            kst[0:KR, G * g + hd, col:col + CH], start=True, stop=True)
                last.then_inc(mx_ps, 1)

            def max_row(v, n_pairs):
                pe.wait_ge(nmx_s, v + 1)
                pe.wait_ge(mx_read, n_pairs)
                nc.tensor.transpose(ps[0:MI, 2, 0:P], nmx[:], ident[:]).then_inc(nmT_ps, 1)

            def unit(u, g, ahead, first=False):
                pe.wait_ge(nm_in, (u + 1) * (16 * NM))
                for t in range(MT):
                    run = (t + LEAD < MI and ahead >= 1) or (t + LEAD >= MI and ahead >= 2)
                    nxt = t + LEAD < MI
                    i = (t + LEAD) % MI
                    v, vg = (u + 1, (g + 1) % NG) if nxt else (u + 2, (g + 2) % NG)
                    if run and i == 0:
                        pe.wait_ge(q_in, (u + 3) * (16 * BLK))
                    pairs = v * (2 * MI) + 2 * i
                    if run:
                        if t == 4 and not first:
                            pe.wait_ge(oT_s, u)
                        maxima(vg, i, 0, pairs)
                    for k in range(G):
                        if k == 0 and not (first and t == 0):
                            pe.wait_ge(p_s, u * (G * MT) + G * t)
                        if k == G - 1:
                            pe.wait_ge(p_s, u * (G * MT) + G * t + 1)
                        if k == 2 and run:
                            if t == 14:
                                pe.wait_ge(nmT_s, u + 2)
                            maxima(vg, i, 1, pairs + 1)
                        nc.tensor.matmul(ps[:, 4 + k % 3, :], kst[0:KR + NM, G * g + k, P * t:P * (t + 1)],
                                         qst[0:KR + NM, g, k, :], start=True, stop=True).then_inc(sc_ps, 1)
                    if t == 3 and not first:
                        pe.wait_ge(o_s, u)
                        if ahead >= 1:
                            pe.wait_ge(mx_read, pairs + 1)
                        for j in range(TPC):
                            last = nc.tensor.transpose(ps[:, 0, P * j:P * (j + 1)], o_sb[:, P * j:P * (j + 1)], ident[:])
                        last.then_inc(oT_ps, 1)
                    if t == 13 and ahead >= 1:
                        max_row(u + 1, (u + 2) * (2 * MI) + (4 if ahead >= 2 else 0))
                    if t == 0 and not first:
                        weigh((g - 1) % NG, MT - 1)
                    if t >= 1:
                        if t == 1 and not first:
                            pe.wait_ge(o_s, u)
                        weigh(g, t - 1)

            def weigh(g, t):
                for k in range(G):
                    last = nc.tensor.matmul(ps[VW * k:VW * (k + 1), 7, :], vp[:, t, G * g + k, :], prob[:, t % 2, k, :],
                                            start=t == 0, stop=t == MT - 1)
                last.then_inc(pv_s, 1)

            pe.wait_ge(kst_in[0], 16 * BLK)
            pe.wait_ge(q_in, 16 * BLK)
            pe.wait_ge(q32_s, 2 * KT * NC)
            for i in range(MI):
                for p in range(2):
                    maxima(0, i, p, 2 * i + p)
            max_row(0, 2 * MI)
            pe.wait_ge(kst_in[1], 16 * BLK)
            pe.wait_ge(q_in, 16 * BLK * 2)
            for i in range(LEAD):
                for p in range(2):
                    if i == 0 and p == 1:
                        pe.wait_ge(nmT_s, 1)
                    maxima(1, i, p, 2 * MI + 2 * i + p)
            pe.wait_ge(v_s, MT // 2)
            pe.wait_ge(vconst, 1)
            pe.wait_ge(kst_one, 1)
            pe.wait_ge(kst_in[2], 32 * BLK)
            unit(0, 0, 2, first=True)
            with pe.Fori(0, NC - 1) as c:
                for g in range(1, NG + 1):
                    unit(c * NG + g, g % NG, 2)
            for g in range(1, NG):
                unit(NU - NG + g, g, min(2, NG - 1 - g))
            pe.wait_ge(p_s, NU * G * MT)
            weigh(NG - 1, MT - 1)
            pe.wait_ge(o_s, NU)
            pe.wait_ge(oT_s, NU - 1)
            for j in range(TPC):
                last = nc.tensor.transpose(ps[:, 0, P * j:P * (j + 1)], o_sb[:, P * j:P * (j + 1)], ident[:])
            last.then_inc(oT_ps, 1)

            pe.wait_ge(mod1_in, 16)
            pe.wait_ge(cb_ready, 2)
            modulation(1)
            pe.wait_ge(oT_s, NU)
            for c in range(NC):
                transposes(1, c)
            pe.wait_ge(hT_s, KT * ln(2, 0))
            for t in range(NT):
                for k in range(KT):
                    last = nc.tensor.matmul(ps[:, 2, E * t:E * (t + 1)], hT[:, k, P * t:P * (t + 1)], rw[:, k, :],
                                            start=k == 0, stop=k == KT - 1)
            last.then_inc(lg_ps, 1)
            pe.wait_ge(ce_s, 1)
            for c in range(NC):
                if c >= 2:
                    pe.wait_ge(ceT_s, c - 1)
                for j in range(TPC):
                    last = nc.tensor.transpose(ps[0:E, c % 2, P * j:P * (j + 1)], lg[:, TPC * c + j, :], ident[:])
                last.then_inc(ce_ps, 1)
            pe.wait_ge(ceT_s, NC)
            pe.wait_ge(sel_s, 1)
            for n, count in enumerate((48, 48, 48)):
                pe.wait_ge(ffw_in[n], count)
            pe.wait_ge(mrow_ready, 2)
            with pe.Fori(0, NC) as c:
                def down(it):
                    rows = P if it < NI - 1 else LAST
                    pe.wait_ge(hid_s, c * NI + it + 1)
                    for j in range(TPC):
                        last = nc.tensor.matmul(ps[:, 6 + j // 2, D * (j % 2):D * (j % 2 + 1)],
                                                hid[0:rows, it % 2, P * j:P * (j + 1)], wd_sb[0:rows, it, :],
                                                start=it == 0 and j % 2 == 0, stop=it == NI - 1, skip_group_check=True)
                    last.then_inc(hid_used, 1)

                for it in range(NI):
                    rows = P if it < NI - 1 else LAST
                    if it >= 2:
                        pe.wait_ge(hid_s, c * NI + it - 1)
                    for w, b in ((wg_sb, 0), (wu_sb, 2)):
                        for k in range(KT):
                            last = nc.tensor.matmul(ps[0:rows, b + it % 2, :], w[:, k, P * it:P * it + rows],
                                                    hT[:, k, bass.ts(c, CH)], start=k == 0, stop=k == KT - 1)
                    last.then_inc(gu_ps, 1)
                    if it < IE:
                        nc.tensor.matmul(ps[:, 4 + it % 2, :], sel[:, P * it:P * (it + 1)], ceT[:, bass.ts(c, CH)],
                                         start=True, stop=True).then_inc(cb_ps, 1)
                    if it >= 1:
                        down(it - 1)
                down(NI - 1)

            pe.wait_ge(y_s, NC)
            pe.wait_ge(y_read, NC)
            transposes(2, 0)
            pe.wait_ge(ux_s, 1)
            for n, w in enumerate((BT_sb, CT_sb)):
                last = nc.tensor.matmul(ps[0:DX, 2, D * n:D * (n + 1)], w[:], ux[:], start=True, stop=True)
            last.then_inc(uw_ps, 1)
            for c in range(1, NC):
                transposes(2, c)
            pe.wait_ge(uw_s, 1)
            for n in range(KT):
                last = nc.tensor.matmul(ps[:, 3, D * n:D * (n + 1)], uu[:, P * n:P * (n + 1)], ww[:], start=True, stop=True)
            last.then_inc(s1_ps, 1)
            pe.wait_ge(bw_s, 1)
            for k in range(KT):
                for o in range(KT):
                    last = nc.tensor.transpose(ps[:, 4, P * (KT * k + o):P * (KT * k + o + 1)],
                                               bw[:, o, P * k:P * (k + 1)], ident[:])
            last.then_inc(bwT_ps, 1)
            pe.wait_ge(att_z, 1)
            pe.wait_ge(hT_s, KT * ln(3, 0))
            for t in range(NT):
                if t >= 2:
                    pe.wait_ge(za_read, t - 1)
                for k in range(KT):
                    last = nc.tensor.matmul(ps[:, 5 + t % 2, 0:D], hT[:, k, P * t:P * (t + 1)], att[:, k, :],
                                            start=k == 0, stop=k == KT - 1)
                last.then_inc(za_ps, 1)
                if t == 1:
                    pe.wait_ge(xa_s, 1)
                    nc.tensor.matmul(ps[0:DX, 7, 0:D], AT_sb[:], xa[:], start=True, stop=True).then_inc(axa_ps, 1)
            def feed(c):
                pe.wait_ge(hT_s, KT * (ln(3, c) + 1))
                for j in range(TPC):
                    t = TPC * c + j
                    if t >= 2:
                        pe.wait_ge(f_read, t - 1)
                    else:
                        pe.wait_ge(uw_s, 1)
                        pe.wait_ge(relu_s, 1)
                    for k in range(KT):
                        last = nc.tensor.matmul(ps[:, 2 + t % 2, 0:D], hT[:, k, P * t:P * (t + 1)], bwT[:, k, :],
                                                start=k == 0, stop=k == KT - 1)
                    last.then_inc(f_ps, 1)

            pe.wait_ge(bwT_s, 1)
            transposes(3, 0)
            for c in range(1, NC):
                transposes(3, c)
                feed(c - 1)
            feed(NC - 1)

        @block.scalar
        def _(act):
            act.dma_start(c_col[0][:], c0.rearrange("o (k p) -> p (o k)", p=P), allow_slow_non_contiguous=True).then_inc(mod_in, 16)
            act.dma_start(wmod_sb[:], wmod0.rearrange("(k p) n -> p k n", p=P)).then_inc(mod_in, 16)
            small = [(bk_col[:], bk.rearrange("(k p) -> p k", p=P)), (bq_col[:], bq.rearrange("(k p) -> p k", p=P)),
                     (c_col[1][:], c1.rearrange("o (k p) -> p (o k)", p=P)),
                     (rw[:], routerT.rearrange("(k p) e -> p k e", p=P)),
                     (AT_sb[:], AT), (BT_sb[:], BT), (CT_sb[:], CT), (r_col[:], r_l.unsqueeze(0).to_broadcast([P, 1]))]
            for dst, src in small:
                act.dma_start(dst, src, allow_slow_non_contiguous=True).then_inc(small_in, 16)
            act.wait_ge(bias0, 1)
            n_small = len(small)
            for b_sb, b in ((bg, sg_b), (bu, su_b)):
                act.dma_start(b_sb[:, IE:NI - 1], b[0:(NI - 1 - IE) * P].rearrange("(t p) -> p t", p=P),
                              allow_slow_non_contiguous=True).then_inc(small_in, 16)
                act.dma_start(b_sb[0:LAST, NI - 1:NI], b[(NI - 1 - IE) * P:SI].unsqueeze(1)).then_inc(small_in, 16)
            act.wait_ge(mod_in, 32)
            act.wait_ge(small_in, 16 * (n_small + 4))
            for n in range(2):
                last = nc.scalar.activation(c_sil[n][:], c_col[n][:], ACT.Silu)
            last.then_inc(c_ready, 1)
            act.wait_ge(consts, 1)

            def deviation(n, c):
                q = ln(n, c)
                act.wait_ge(var_s, TPC * (q + 1))
                act.wait_ge(rs_s, q)
                nc.scalar.activation(std[:], mvs[n][:, TPC * c:TPC * (c + 1), 1], ACT.Sqrt, bias=eps[:, 0:1]).then_inc(std_s, 1)

            def modulate(n, c):
                q = ln(n, c)
                first = 0 if n % 2 == 0 else 6
                for ft in range(KT):
                    act.wait_ge(tr_ps, KT * q + ft + 1)
                    nc.scalar.activation(hT[:, ft, CH * c:CH * (c + 1)], ps[:, ft, :], ACT.Identity,
                                         scale=mcol[n // 2][:, first + 2 + ft:first + 3 + ft],
                                         bias=mcol[n // 2][:, first + ft:first + 1 + ft]).then_inc(hT_s, 1)

            def proj(i, b_col, ft):
                act.wait_ge(proj_ps, i + 1)
                if i >= 2:
                    act.wait_ge(split_s, i - 1)
                nc.scalar.activation(q32[:, i % 2, :], ps[:, 2 + i % 2, :], ACT.Identity,
                                     bias=b_col[:, ft:ft + 1]).then_inc(q32_s, 1)

            deviation(0, 0)
            deviation(0, 1)
            act.wait_ge(mcol_ready, 1)
            modulate(0, 0)
            for c in range(1, NC):
                if c + 1 < NC:
                    deviation(0, c + 1)
                modulate(0, c)
                for ft in range(KT):
                    proj(KT * (c - 1) + ft, bk_col, ft)
            for ft in range(KT):
                proj(KT * (NC - 1) + ft, bk_col, ft)
            for c in range(NC):
                for ft in range(KT):
                    proj(KT * NC + KT * c + ft, bq_col, ft)

            def max_rows(v):
                act.wait_ge(nmT_ps, v + 1)
                act.wait_ge(nm_s, v)
                nc.scalar.activation(nm32[:], ps[0:MI, 2, 0:P], ACT.Copy).then_inc(nmT_s, 1)

            def leave_output(u):
                act.wait_ge(pv_s, (u + 1) * MT)
                nc.scalar.activation(o_sb[:], ps[:, 7, :], ACT.Copy).then_inc(o_s, 1)

            def leave_transposed(u):
                act.wait_ge(oT_ps, u + 1)
                if isinstance(u, int) and u == NU - 1:
                    act.wait_ge(att_s, u)
                else:
                    act.wait_ge(nm_s, u + 2)
                nc.scalar.activation(o_tm[:].rearrange("p j k w -> p (j k w)"), ps[:, 0, :], ACT.Copy).then_inc(oT_s, 1)

            def unit(u, first, ahead):
                for t in range(MT):
                    if t == 1 and not first:
                        leave_output(u - 1)
                    if t == 4 and not first:
                        leave_transposed(u - 1)
                    if t == 14 and ahead >= 1:
                        max_rows(u + 1)
                    for k in range(G):
                        act.wait_ge(sc_ps, u * (G * MT) + G * t + k + 1)
                        if k == 0 and not (first and t < 2):
                            act.wait_ge(pv_s, u * MT + t - 1)
                        nc.scalar.activation(prob[:, t % 2, k, :], ps[:, 4 + k % 3, :], ACT.Exp,
                                             scale=DH ** -0.5).then_inc(p_s, 1)

            max_rows(0)
            act.wait_ge(kd_out, 16 * KT * NC)
            unit(0, True, 2)
            with act.Fori(1, NU - 2) as u:
                unit(u, False, 2)
            unit(NU - 2, False, 1)
            unit(NU - 1, False, 0)
            leave_output(NU - 1)
            leave_transposed(NU - 1)

            for c in range(NC):
                deviation(1, c)
                if c == 0:
                    act.wait_ge(mcol_ready, 1)
                modulate(1, c)
            act.wait_ge(rt, 2)
            nc.scalar.activation(pr[:], lg[:], ACT.Exp).then_inc(exp_s, 1)
            with act.Fori(0, NC) as c:
                for it in range(NI):
                    rows = P if it < NI - 1 else LAST
                    act.wait_ge(gu_ps, c * NI + it + 1)
                    if it >= 2:
                        act.wait_ge(hid_s, c * NI + it - 1)
                    nc.scalar.activation(sig[0:rows, it % 2, :], ps[0:rows, it % 2, :], ACT.Silu,
                                         bias=bg[0:rows, it:it + 1]).then_inc(sig_s, 1)
            for c in range(NC):
                deviation(2, c)
                modulate(2, c)
            act.wait_ge(s1_ps, 1)
            nc.scalar.activation(att[:].rearrange("p k m -> p (k m)"), ps[:, 3, :], ACT.Relu).then_inc(relu_s, 1)
            for c in range(NC):
                deviation(3, c)
                modulate(3, c)

        @block.vector
        def _(dve):
            steps = [0]

            def then(ins):
                steps[0] += 1
                ins.then_inc(rows_step, 1)
                dve.wait_ge(rows_step, steps[0])

            for b_sb in (bg, bu):
                last = nc.vector.memset(b_sb[:], 0.0)
            last.then_inc(bias0, 1)

            def statistics(n, c):
                q = ln(n, c)
                if q >= 1:
                    dve.wait_ge(var_s, TPC * q)
                for j in range(TPC):
                    nc.vector.bn_stats(bn_st[:, j, :], x[:, TPC * c + j, :]).then_inc(bn_s, 1)
                dve.wait_ge(bn_s, TPC * (q + 1))
                for j in range(TPC):
                    nc.vector.bn_aggr(mvs[n][:, TPC * c + j, :], bn_st[:, j, :]).then_inc(var_s, 1)

            def normalise(n, c):
                q = ln(n, c)
                dve.wait_ge(std_s, q + 1)
                nc.vector.reciprocal(rss[n][:, TPC * c:TPC * (c + 1)], std[:]).then_inc(rs_s, 1)
                dve.wait_ge(rs_s, q + 1)
                if q >= 2:
                    dve.wait_ge(tr_ps, KT * (q - 1))
                for j in range(TPC):
                    t = TPC * c + j
                    nc.vector.tensor_scalar(xh[:, q % 2, j, :], x[:, t, :], mvs[n][:, t, 0:1], rss[n][:, t:t + 1],
                                            ALU.subtract, ALU.mult).then_inc(xh_s, 1)

            def broadcast_c(n):
                for k in range(KT):
                    last = nc.vector.tensor_copy(cb[:, k, :], c_sil[n][:, k:k + 1].to_broadcast([P, P]))
                last.then_inc(cb_ready, 1)

            def columns(n):
                dve.wait_ge(mcol_ps, n + 1)
                then(nc.vector.tensor_copy(mcol[n][:], ps[:, 7, 0:12]))
                for a in (2, 8):
                    last = nc.vector.tensor_scalar(mcol[n][:, a:a + 2], mcol[n][:, a:a + 2], 1.0, None, ALU.add)
                last.then_inc(mcol_ready, 1)

            def gate_row(dst, src, tmp):
                then(nc.vector.tensor_scalar(tmp, src, 0.0, 2.0, ALU.is_ge, ALU.mult))
                then(nc.vector.scalar_tensor_tensor(dst, src, -1.0, src, ALU.mult, ALU.max))
                then(nc.vector.tensor_scalar(dst, dst, 0.25, None, ALU.max))
                then(nc.vector.scalar_tensor_tensor(dst, tmp, -1.0, dst, ALU.add, ALU.mult))

            def modulation_rows(n, rows):
                dve.wait_ge(mrow_ps, n + 1)
                for j in range(3):
                    ins = nc.vector.tensor_copy(mrow[:, 2 * j:2 * j + 2, :].rearrange("p a d -> p (a d)"), ps[:, 4 + j, :])
                then(ins)
                gate_row(rows[:, GA, :], mrow[:, 2, :], rows[:, GCA, :])
                gate_row(rows[:, GB, :], mrow[:, 5, :], rows[:, GCA, :])
                then(nc.vector.scalar_tensor_tensor(rows[:, GCA, :], mrow[:, 1, :], 1.0, rows[:, GA, :], ALU.add, ALU.mult))
                then(nc.vector.tensor_tensor(rows[:, GSA, :], mrow[:, 0, :], rows[:, GA, :], ALU.mult))

            def split(i, parts, ft, c):
                b, cols = i % 2, slice(CH * c, CH * (c + 1))
                dve.wait_ge(q32_s, i + 1)
                nc.vector.tensor_copy(parts[:, ft, 0, cols], q32[:, b, :]).then_inc(hi_s, 1)
                dve.wait_ge(hi_s, i + 1)
                nc.vector.tensor_tensor(res[:, b, :], q32[:, b, :], parts[:, ft, 0, cols], ALU.subtract).then_inc(r_s, 1)
                dve.wait_ge(r_s, i + 1)
                nc.vector.tensor_copy(parts[:, ft, 1, cols], res[:, b, :]).then_inc(mid_s, 1)
                dve.wait_ge(mid_s, i + 1)
                nc.vector.tensor_tensor(parts[:, ft, 2, cols], res[:, b, :], parts[:, ft, 1, cols],
                                        ALU.subtract).then_inc(split_s, 1)

            dve.wait_ge(x_in_s[0], 16)
            statistics(0, 0)
            dve.wait_ge(c_ready, 1)
            broadcast_c(0)
            columns(0)
            normalise(0, 0)
            dve.wait_ge(x_in_s[1], 16)
            statistics(0, 1)
            normalise(0, 1)
            modulation_rows(0, rows0)
            nc.vector.tensor_copy(rows0[:, GSA, :], rows0[:, GSA, :]).then_inc(mrow_ready, 1)
            for c in range(2, NC):
                dve.wait_ge(x_in_s[c], 16)
                statistics(0, c)
                normalise(0, c)
                for ft in range(KT):
                    split(KT * (c - 2) + ft, kp, ft, c - 2)
            for c in range(2, NC):
                for ft in range(KT):
                    split(KT * c + ft, kp, ft, c)
            for c in range(NC):
                for ft in range(KT):
                    split(KT * NC + KT * c + ft, qp, ft, c)
            dve.wait_ge(wv_in, 32)
            dve.wait_ge(vconst, 1)
            for i in range(MT // 2):
                dve.wait_ge(v_ps, i + 1)
                nc.vector.tensor_tensor(vp[:, 2 * i:2 * i + 2, :, 0:DH],
                                        ps[:, 4 + i % 2, :].rearrange("p (j h d) -> p j h d", j=2, h=H),
                                        bv_row[:].rearrange("p (h d) -> p h d", h=H).unsqueeze(1).to_broadcast([P, 2, H, DH]),
                                        ALU.add).then_inc(v_s, 1)

            def reduce_pair(i, p, n):
                dve.wait_ge(mx_ps, n + 1)
                nc.vector.tensor_reduce(mxp[:, i, p:p + 1], ps[:, 2 * p:2 * p + 2, :], AX.XY, ALU.max).then_inc(mx_read, 1)

            def negative_max(v):
                dve.wait_ge(mx_read, (v + 1) * (2 * MI))
                dve.wait_ge(nmT_ps, v)
                nc.vector.tensor_reduce(nmx[:], mxp[:], AX.X, ALU.max, negate=True).then_inc(nmx_s, 1)

            def invert_sums(u):
                dve.wait_ge(oT_s, u + 1)
                nc.vector.reciprocal(rec[:], o_tm[:, :, :, DH]).then_inc(rec_s, 1)

            def unit(u, first, ahead):
                for t in range(MT):
                    i = (t + LEAD) % MI
                    v = u + 1 if t + LEAD < MI else u + 2
                    run = (t + LEAD < MI and ahead >= 1) or (t + LEAD >= MI and ahead >= 2)
                    if run:
                        for p in range(2):
                            if i == 0 and p == 0:
                                dve.wait_ge(nmx_s, v)
                            reduce_pair(i, p, v * (2 * MI) + 2 * i + p)
                    if t + LEAD == MI - 1 and ahead >= 1:
                        negative_max(u + 1)
                    if t == 5 and not first:
                        invert_sums(u - 1)

            for i in range(MI):
                for p in range(2):
                    reduce_pair(i, p, 2 * i + p)
            negative_max(0)
            dve.wait_ge(nmx_s, 1)
            for i in range(LEAD):
                for p in range(2):
                    reduce_pair(i, p, 2 * MI + 2 * i + p)
            unit(0, True, 2)
            with dve.Fori(1, NU - 2) as u:
                unit(u, False, 2)
            unit(NU - 2, False, 1)
            unit(NU - 1, False, 0)
            invert_sums(NU - 1)

            dve.wait_ge(pv_s, MT * NU)
            broadcast_c(1)
            dve.wait_ge(att_s, NU)
            columns(1)
            modulation_rows(1, rows1)
            then(nc.vector.tensor_scalar(rows1[:, RGA, :], rows1[:, GA, :], r_col[:, 0:1], None, ALU.mult))
            dve.wait_ge(l1_in, 48)
            nc.vector.tensor_tensor(gsd[:], sdb_row[:], rows0[:, GB, :], ALU.mult)
            nc.vector.tensor_tensor(gb1[:], b1_row[:], rows1[:, GB, :], ALU.mult).then_inc(mrow_ready, 1)
            for c in range(NC):
                statistics(1, c)
                normalise(1, c)

            dve.wait_ge(lg_ps, 1)
            then(nc.vector.tensor_reduce(r16[:], ps[:, 2, 0:NT * E].rearrange("p (t e) -> p t e", e=E), AX.X, ALU.max))
            rt_n = [0]

            def rt_then(ins):
                rt_n[0] += 1
                ins.then_inc(rt, 1)
                dve.wait_ge(rt, rt_n[0])

            rt_then(nc.vector.tensor_copy(lg[:], ps[:, 2, 0:NT * E].rearrange("p (t e) -> p t e", e=E)))
            rt_then(nc.vector.tensor_tensor(lg[:], lg[:], r16[:].unsqueeze(2).to_broadcast([P, NT, E]), ALU.subtract))
            dve.wait_ge(exp_s, 1)
            rt_then(nc.vector.tensor_reduce(r16[:], pr[:], AX.X, ALU.add))
            rt_then(nc.vector.reciprocal(r16b[:], r16[:]))
            rt_then(nc.vector.tensor_tensor(pr[:], pr[:], r16b[:].unsqueeze(2).to_broadcast([P, NT, E]), ALU.mult))
            other = pr[:].unsqueeze(2).to_broadcast([P, NT, E, E])
            own = pr[:].unsqueeze(3).to_broadcast([P, NT, E, E])
            nc.vector.tensor_tensor(cmp1[:], other, own, ALU.is_gt)
            rt_then(nc.vector.tensor_tensor(cmp2[:], other, own, ALU.is_equal))
            dve.wait_ge(sel_s, 1)
            rt_then(nc.vector.tensor_tensor(cmp2[:], cmp2[:], tri[:].unsqueeze(1).to_broadcast([P, NT, E, E]), ALU.mult))
            rt_then(nc.vector.tensor_tensor(cmp1[:], cmp1[:], cmp2[:], ALU.add))
            rt_then(nc.vector.tensor_reduce(rank[:], cmp1[:], AX.X, ALU.add))
            rt_then(nc.vector.scalar_tensor_tensor(lg[:], rank[:], 2.0, pr[:], ALU.is_lt, ALU.mult))
            rt_then(nc.vector.tensor_reduce(r16[:], lg[:], AX.X, ALU.add))
            rt_then(nc.vector.reciprocal(r16b[:], r16[:]))
            nc.vector.tensor_tensor(lg[:], lg[:], r16b[:].unsqueeze(2).to_broadcast([P, NT, E]), ALU.mult).then_inc(ce_s, 1)
            for c in range(NC):
                dve.wait_ge(ce_ps, c + 1)
                nc.vector.tensor_copy(ceT[:, CH * c:CH * (c + 1)], ps[0:E, c % 2, :]).then_inc(ceT_s, 1)

            dve.wait_ge(xsd_s, NT)
            with dve.Fori(0, NC) as c:
                for it in range(NI):
                    rows = P if it < NI - 1 else LAST
                    dve.wait_ge(sig_s, c * NI + it + 1)
                    up, sg, hd = ps[0:rows, 2 + it % 2, :], sig[0:rows, it % 2, :], hid[0:rows, it % 2, :]
                    if it < IE:
                        if it >= 2:
                            dve.wait_ge(hid_s, c * NI + it - 1)
                        nc.vector.scalar_tensor_tensor(tmul[:, it % 2, :], up, bu[:, it:it + 1], sg, ALU.add, ALU.mult).then_inc(t_s, 1)
                        dve.wait_ge(t_s, c * IE + it + 1)
                        dve.wait_ge(cb_ps, c * IE + it + 1)
                        if it >= 2:
                            dve.wait_ge(hid_used, c * NI + it - 1)
                        nc.vector.tensor_tensor(hd, ps[:, 4 + it % 2, :], tmul[:, it % 2, :], ALU.mult).then_inc(hid_s, 1)
                    else:
                        dve.wait_ge(hid_used, c * NI + it - 1)
                        nc.vector.scalar_tensor_tensor(hd, up, bu[0:rows, it:it + 1], sg, ALU.add, ALU.mult).then_inc(hid_s, 1)
                dve.wait_ge(hid_used, (c + 1) * NI)
                gb = rows0[:, GB, :].unsqueeze(1).to_broadcast([P, TPC, D])
                nc.vector.tensor_tensor(yt[:], ps[:, 6:8, :].rearrange("p b (j d) -> p (b j) d", j=2), gb,
                                        ALU.mult).then_inc(y_read, 1)
                dve.wait_ge(y_read, c + 1)
                x_c = x[:, bass.ds(c * TPC, TPC), :]
                nc.vector.tensor_tensor(x_c, x_c, yt[:], ALU.add).then_inc(y_s, 1)

            for c in range(NC):
                dve.wait_ge(y_s, c + 1)
                statistics(2, c)
                if c >= 2:
                    dve.wait_ge(res1_s, TPC * (c - 1))
                normalise(2, c)
                if c == 0:
                    dve.wait_ge(xh_s, TPC * (ln(2, 0) + 1))
                    then(nc.vector.scalar_tensor_tensor(ux[:], mrow[0:DX, 1, :], 1.0, xh[0:DX, 0, 0, :], ALU.add, ALU.mult))
                    nc.vector.tensor_tensor(ux[:], ux[:], mrow[0:DX, 0, :], ALU.add).then_inc(ux_s, 1)
            dve.wait_ge(uw_ps, 1)
            nc.vector.tensor_copy(uu[:], ps[0:DX, 2, 0:D])
            nc.vector.tensor_copy(ww[:], ps[0:DX, 2, D:2 * D]).then_inc(uw_s, 1)
            then(nc.vector.tensor_reduce(alpha[:], w1_sb[:], AX.X, ALU.add, apply_absolute_value=True))
            then(nc.vector.tensor_scalar(alpha[:], alpha[:], 1.0 / D, None, ALU.mult))
            then(nc.vector.tensor_scalar(bw[:], w1_sb[:], 0.0, 2.0, ALU.is_ge, ALU.mult))
            for k in range(KT):
                ins = nc.vector.tensor_scalar(bw[:, k, :], bw[:, k, :], -1.0, alpha[:, k:k + 1], ALU.add, ALU.mult)
            then(ins)
            then(nc.vector.tensor_tensor(bw[:], bw[:], w1_sb[:], ALU.subtract))
            nc.vector.tensor_tensor(bw[:], bw[:], w1_sb[:], ALU.add).then_inc(bw_s, 1)
            dve.wait_ge(bwT_ps, 1)
            nc.vector.tensor_copy(bwT[:].rearrange("p k o -> p (k o)"), ps[:, 4, :]).then_inc(bwT_s, 1)

            dve.wait_ge(res1_s, NT)
            for t in range(NT):
                b = ps[:, 5 + t % 2, 0:D]
                dve.wait_ge(za_ps, t + 1)
                if t >= 2:
                    dve.wait_ge(za_s, t - 1)
                if t == 0:
                    nc.vector.tensor_copy(xa[:], b[0:DX]).then_inc(xa_s, 1)
                    nc.vector.tensor_tensor(yt2[32:64, 0, :], b[32:64], rows1[32:64, RGA, :], ALU.mult)
                    nc.vector.tensor_tensor(yt2[64:128, 0, :], b[64:128], rows1[64:128, RGA, :], ALU.mult).then_inc(za_read, 1)
                    dve.wait_ge(axa_ps, 1)
                    nc.vector.tensor_tensor(yt2[0:DX, 0, :], ps[0:DX, 7, 0:D], rows1[0:DX, GA, :], ALU.mult).then_inc(axa_s, 1)
                    dve.wait_ge(axa_s, 1)
                else:
                    nc.vector.tensor_tensor(yt2[:, t % 2, :], b, rows1[:, RGA, :], ALU.mult).then_inc(za_read, 1)
                dve.wait_ge(za_read, t + 1)
                nc.vector.tensor_tensor(x[:, t, :], x[:, t, :], yt2[:, t % 2, :], ALU.add).then_inc(za_s, 1)
            def add_feed(c):
                for t in range(TPC * c, TPC * (c + 1)):
                    dve.wait_ge(xb_s, t + 1)
                    dve.wait_ge(f_ps, t + 1)
                    if t >= 2:
                        dve.wait_ge(f_s, t - 1)
                    nc.vector.tensor_tensor(yt2[:, t % 2, :], ps[:, 2 + t % 2, 0:D], rows1[:, GB, :], ALU.mult).then_inc(f_read, 1)
                    dve.wait_ge(f_read, t + 1)
                    nc.vector.tensor_tensor(x[:, t, :], x[:, t, :], yt2[:, t % 2, :], ALU.add).then_inc(f_s, 1)

            for c in range(NC):
                dve.wait_ge(za_s, TPC * (c + 1))
                statistics(3, c)
                normalise(3, c)
                if c >= 1:
                    add_feed(c - 1)
            add_feed(NC - 1)

        @block.gpsimd
        def _(pool):
            setup = [0]

            def then(ins):
                setup[0] += 1
                ins.then_inc(res_step, 1)
                pool.wait_ge(res_step, setup[0])

            nc.gpsimd.memset(eps[:], EPS)
            then(nc.gpsimd.memset(ident[:], 0.0))
            nc.gpsimd.affine_select(ident[:], ident[:], [[-1, P]], ALU.not_equal, 1.0, base=0,
                                    channel_multiplier=1).then_inc(consts, 1)
            pool.wait_ge(consts, 1)
            one_pair = struct.unpack("<f", struct.pack("<I", 0x3F803F80))[0]
            nc.gpsimd.memset(kst[KR:KR + NM].rearrange("p h t -> p (h t)").bitcast(F32), one_pair).then_inc(kst_one, 1)
            pool.wait_ge(kst_one, 1)
            pool.wait_ge(proj_ps, 2 * KT * NC)
            pool.wait_ge(mrow_ready, 1)
            nc.gpsimd.memset(vp[:, :, :, DH + 1:VW], 0.0)
            nc.gpsimd.memset(vp[:, :, :, DH], 1.0).then_inc(vconst, 1)
            pool.wait_ge(vconst, 1)

            def split_max(v):
                pool.wait_ge(nmT_s, v + 1)
                pool.wait_ge(nm_in, v * (16 * NM))
                nc.gpsimd.tensor_copy(nmp[:, 0, :], nm32[:]).then_inc(nm_step, 1)
                pool.wait_ge(nm_step, v * 3 + 1)
                nc.gpsimd.tensor_tensor(nmr[:], nm32[:], nmp[:, 0, :], ALU.subtract).then_inc(nm_step, 1)
                pool.wait_ge(nm_step, v * 3 + 2)
                nc.gpsimd.tensor_copy(nmp[:, 1, :], nmr[:]).then_inc(nm_step, 1)
                pool.wait_ge(nm_step, v * 3 + 3)
                nc.gpsimd.tensor_tensor(nmp[:, 2, :], nmr[:], nmp[:, 1, :], ALU.subtract).then_inc(nm_s, 1)

            def residual(lo, hi):
                for t in range(lo, hi):
                    then(nc.gpsimd.tensor_scalar(xt[:], x[:, t, :], mvs[0][:, t, 0:1], rss[0][:, t:t + 1],
                                                 ALU.subtract, ALU.mult))
                    then(nc.gpsimd.tensor_tensor(xt[:], xt[:], rows0[:, GCA, :], ALU.mult))
                    then(nc.gpsimd.tensor_tensor(xt[:], xt[:], rows0[:, GSA, :], ALU.add))
                    then(nc.gpsimd.tensor_tensor(x[:, t, :], x[:, t, :], xt[:], ALU.add))

            def add_attention(u, c, g):
                pool.wait_ge(rec_s, u + 1)
                nc.gpsimd.tensor_tensor(att_u[:], o_tm[:, :, :, 0:DH], rec[:].unsqueeze(3).to_broadcast([P, TPC, G, DH]),
                                        ALU.mult).then_inc(att_step, 1)
                pool.wait_ge(att_step, u * 2 + 1)
                w = G * DH
                flat = att_u[:].rearrange("p j k d -> p j (k d)")
                nc.gpsimd.tensor_tensor(flat, flat, rows0[:, GA, w * g:w * (g + 1)].unsqueeze(1).to_broadcast([P, TPC, w]),
                                        ALU.mult).then_inc(att_step, 1)
                pool.wait_ge(att_step, u * 2 + 2)
                dst = x[:, c * TPC:(c + 1) * TPC, w * g:w * (g + 1)]
                nc.gpsimd.tensor_tensor(dst, dst, flat, ALU.add).then_inc(att_s, 1)

            split_max(0)
            pool.wait_ge(nm_s, 1)
            pool.wait_ge(split_s, KT * NC)
            pool.wait_ge(kd_out, 16 * KT * NC)
            residual(0, NT // 2)
            split_max(1)
            pool.wait_ge(nm_s, 2)
            residual(NT // 2, NT)
            for u in range(NU):
                add_attention(u, u // NG, u % NG)
                pool.wait_ge(att_s, u + 1)
                if u + 2 < NU:
                    split_max(u + 2)
                    pool.wait_ge(nm_s, u + 3)
            pool.wait_ge(qd_out, 16 * KT * NC)
            then(nc.gpsimd.memset(tri[:], 1.0))
            then(nc.gpsimd.memset(sel[:], 1.0))
            then(nc.gpsimd.affine_select(tri[:], tri[:], [[1, E], [-1, E]], ALU.is_gt, 0.0, base=0, channel_multiplier=0))
            then(nc.gpsimd.affine_select(sel[:], sel[:], [[1, E * I]], ALU.is_ge, 0.0, base=0, channel_multiplier=-I))
            nc.gpsimd.affine_select(sel[:], sel[:], [[-1, E * I]], ALU.is_ge, 0.0, base=I - 1,
                                    channel_multiplier=I).then_inc(sel_s, 1)
            pool.wait_ge(mrow_ready, 2)
            pool.wait_ge(xh_s, TPC * ln(2, 0))
            for t in range(NT):
                nc.gpsimd.tensor_tensor(x[:, t, :], x[:, t, :], gsd[:], ALU.add).then_inc(xsd_s, 1)
            pool.wait_ge(xsd_s, NT)
            for t in range(NT):
                q = ln(2, 0) * TPC + t
                pool.wait_ge(xh_s, q + 1)
                if t >= 1:
                    pool.wait_ge(res1_s, t)
                xh_t = xh[:, (t // TPC) % 2, t % TPC, :]
                nc.gpsimd.tensor_tensor(xt[:], xh_t, rows1[:, GCA, :], ALU.mult).then_inc(res1_step, 1)
                pool.wait_ge(res1_step, 2 * t + 1)
                nc.gpsimd.tensor_tensor(xt[:], xt[:], rows1[:, GSA, :], ALU.add).then_inc(res1_step, 1)
                pool.wait_ge(res1_step, 2 * t + 2)
                nc.gpsimd.tensor_tensor(x[:, t, :], x[:, t, :], xt[:], ALU.add).then_inc(res1_s, 1)
            pool.wait_ge(relu_s, 1)
            nc.gpsimd.affine_select(att[:, KT - 1, :], att[:, KT - 1, :], [[1, D]], ALU.not_equal, 0.0,
                                    base=-((P - 1) * D + D - 1), channel_multiplier=D).then_inc(att_z, 1)
            for t in range(NT):
                pool.wait_ge(xh_s, TPC * ln(3, 0) + t + 1)
                nc.gpsimd.tensor_tensor(x[:, t, :], x[:, t, :], gb1[:], ALU.add).then_inc(xb_s, 1)

    return nc


def kernel(L0_attn_x, L0_attn_Wq, L0_attn_bq, L0_attn_Wk, L0_attn_bk, L0_attn_Wv, L0_attn_bv, L0_ffn_router_w,
           L0_ffn_gate_w, L0_ffn_up_w, L0_ffn_down_w, L0_ffn_s_gate_w, L0_ffn_s_gate_b, L0_ffn_s_up_w,
           L0_ffn_s_up_b, L0_ffn_s_down_w, L0_ffn_s_down_b, L0_c, L0_wmod, L1_attn_A_l, L1_attn_r_l, L1_attn_B_l,
           L1_attn_C_l, L1_ffn_weight, L1_ffn_bias, L1_c, L1_wmod):
    import concourse.bacc as bacc
    from concourse.bass_utils import run_bass_kernel_spmd

    laid = [("x", np.asarray(L0_attn_x).reshape(T, D)),
            ("wq", L0_attn_Wq), ("bq", L0_attn_bq), ("wk", L0_attn_Wk), ("bk", L0_attn_bk), ("wv", L0_attn_Wv),
            ("bv", L0_attn_bv), ("routerT", np.asarray(L0_ffn_router_w).T), ("gate_w", L0_ffn_gate_w),
            ("up_w", L0_ffn_up_w), ("down_w", L0_ffn_down_w), ("sg_w", L0_ffn_s_gate_w), ("sg_b", L0_ffn_s_gate_b),
            ("su_w", L0_ffn_s_up_w), ("su_b", L0_ffn_s_up_b), ("sd_w", L0_ffn_s_down_w), ("sd_b", L0_ffn_s_down_b),
            ("c0", L0_c), ("wmod0", L0_wmod), ("AT", np.asarray(L1_attn_A_l).T), ("r_l", L1_attn_r_l),
            ("BT", np.asarray(L1_attn_B_l).T), ("CT", np.asarray(L1_attn_C_l).T), ("w1", L1_ffn_weight),
            ("b1", L1_ffn_bias), ("c1", L1_c), ("wmod1", L1_wmod)]
    nc = bacc.Bacc("TRN2", target_bir_lowering=False, num_devices=1)
    arrays, args = {}, []
    for name, a in laid:
        arrays[name] = np.ascontiguousarray(a)
        args.append(nc.dram_tensor(name, arrays[name].shape, F32, kind="ExternalInput").ap())
    args.append(nc.dram_tensor("out", (T, D), F32, kind="ExternalOutput").ap())
    build(nc, *args)
    got = run_bass_kernel_spmd(nc, [arrays], core_ids=[0]).results[0]["out"]
    return got.reshape(1, T, D)
```

```python
import struct
from contextlib import ExitStack

import concourse.bass as bass
import numpy as np
from concourse import mybir

F32 = mybir.dt.float32
BF16 = mybir.dt.bfloat16
F32R = mybir.dt.float32r
ALU = mybir.AluOpType
ACT = mybir.ActivationFunctionType
AX = mybir.AxisListType

P = 128
T, D = 2048, 256
KT = D // P
NT = T // P
CH = 512
NC = T // CH
TPC = CH // P
H, DH = 16, 16
G = 4
NG = H // G
NU = NC * NG
MT = T // P
BLK = 6
KR = BLK * DH
NM = 3
Q_PART = (0, 0, 1, 0, 2, 1)
K_PART = (0, 1, 0, 2, 0, 1)
VW = 32
E, I, SI = 8, 176, 352
IE = E * I // P
IA = E * I + SI
NI = -(-IA // P)
LAST = IA - (NI - 1) * P
DX = 32
CR = 32
EARLY = 4
EPS = 1e-5
LEAD = 4
MI = G * TPC


def build(nc, x_in, wq, bq, wk, bk, wv, bv, routerT, gate_w, up_w, down_w, sg_w, sg_b, su_w, su_b,
          sd_w, sd_b, c0, wmod0, AT, r_l, BT, CT, w1, b1, c1, wmod1, out):
    ctx = ExitStack()
    base = -(-nc.sbuf_base // 64) * 64
    top = [base]

    def region(nbytes):
        at = top[0]
        top[0] += -(-nbytes // 32) * 32
        assert top[0] <= nc.sbuf_usable_end, top[0]
        return at

    def at(name, shape, dt, offset):
        return nc.alloc_sbuf_tensor_at(name, shape, dt, offset=offset)

    def new(name, shape, dt=F32):
        n = int(np.prod(shape[1:])) * (2 if dt == BF16 else 4)
        return at(name, shape, dt, region(n))

    with ctx:
        x = new("x", [P, NT, D])
        hT_reg = region(KT * T * 4)
        ident = new("ident", [P, P])
        wv_reg = region((KT + 1) * D * 4)
        wv_sb = at("wv_sb", [P, KT, D], F32, wv_reg)
        bv_row = at("bv_row", [P, D], F32, wv_reg + KT * D * 4)
        sel = at("sel", [3 * CR, E * I], BF16, wv_reg)
        rows0 = new("rows0", [P, 4, D])
        GCA, GSA, GA, GB = range(4)
        mcol = [new(f"mcol{n}", [P, 12]) for n in range(2)]
        mv0, rs0 = new("mv0", [P, NT, 2]), new("rs0", [P, NT])
        mv1, rs1 = new("mv1", [P, TPC, 2]), new("rs1", [P, TPC])
        bn_st = new("bn_st", [P, TPC, 6])
        veps = new("veps", [P, TPC])
        m05 = new("m05", [P, TPC])
        c_col = [new(f"c_col{n}", [P, KT]) for n in range(2)]
        c_sil = [new(f"c_sil{n}", [P, KT]) for n in range(2)]
        bq_col, bk_col = new("bq_col", [P, KT]), new("bk_col", [P, KT])
        mxp = new("mxp", [P, MI, 2])
        nmx = new("nmx", [P, MI])
        nm32, nmr = new("nm32", [MI, P]), new("nmr", [MI, P])
        nmp = new("nmp", [MI, NM, P], BF16)
        rec = new("rec", [P, TPC, G])
        rw = new("rw", [P, KT, E])
        rw_hi, rw_lo = new("rw_hi", [P, KT, E], F32R), new("rw_lo", [P, KT, E], F32R)
        bg, bu = new("bg", [P, NI]), new("bu", [P, NI])
        AT_sb, BT_sb, CT_sb = new("AT_sb", [DX, DX]), new("BT_sb", [DX, DX]), new("CT_sb", [DX, DX])
        r_col = new("r_col", [P, 1])

        k_reg = region(H * T * 2)
        q_reg = region(4 * G * CH * 2)
        qp_reg = region(KT * 3 * T * 2)
        p_reg = region(2 * G * CH * 4)
        e_reg = region(8192)
        v_reg = region(MT * H * VW * 4)

        hT = at("hT", [P, KT, T], F32, hT_reg)
        kst = at("kst", [P, H, T], BF16, k_reg)
        qst = at("qst", [P, 4, G, CH], BF16, q_reg)
        xh = at("xh", [P, 2, TPC, D], F32, q_reg)
        q32 = at("q32", [P, 2, CH], F32, q_reg + 8192)
        res = at("res", [P, 2, CH], F32, q_reg + 8192 + 4096)
        qp = at("qp", [P, KT, 3, T], BF16, qp_reg)
        kp = at("kp", [P, KT, 3, T], BF16, p_reg)
        prob = at("prob", [P, 2, G, CH], F32, p_reg)
        o_sb = at("o_sb", [P, CH], F32, e_reg)
        o_tm = at("o_tm", [P, TPC, G, VW], F32, e_reg + 2048)
        att_u = at("att_u", [P, TPC, G, DH], F32, e_reg + 4096)
        xt = at("xt", [P, D], F32, e_reg + 5120)
        vp = at("vp", [P, MT, H, VW], F32, v_reg)
        wmod_sb = at("wmod_sb", [P, KT, 6 * D], F32, v_reg)
        mrow = at("mrow", [P, 6, D], F32, v_reg + 12288)
        cb = at("cb", [P, KT, P], F32, v_reg + 18432)
        wk_sb = at("wk_sb", [P, KT, D], F32, v_reg + 28672)
        wq_sb = at("wq_sb", [P, KT, D], F32, v_reg + 30720)
        W_B = KT * IA * 4
        SPARE = H * T * 2 // 4
        k0, k1, k2, k3 = (k_reg + SPARE * g for g in range(4))
        wg_raw = at("wg_raw", [P, KT, IA], F32, hT_reg)
        wg_hi, wg_lo = at("wg_hi", [P, KT, IA], F32R, qp_reg), at("wg_lo", [P, KT, IA], F32R, k0)
        wu_raw, wu_lo = at("wu_raw", [P, KT, IA], F32, k1), at("wu_lo", [P, KT, IA], F32R, k1)
        wd_raw, wd_lo = at("wd_raw", [P, NI, D], F32, k2), at("wd_lo", [P, NI, D], F32R, k2)
        wu_hi = at("wu_hi", [P, KT, IA], F32R, v_reg)
        wd_hi = at("wd_hi", [P, NI, D], F32R, v_reg + W_B)
        hTc = at("hTc", [P, KT, CH], F32, v_reg + W_B + NI * D * 4)
        hT_hi = at("hT_hi", [P, KT, T], F32R, hT_reg)
        hT_lo = at("hT_lo", [P, NC * KT * CH], F32R, q_reg)
        sig = at("sig", [P, 2, CH], F32, k3)
        hid = at("hid", [P, 2, CH], F32, k3 + 4096)
        hid_hi, hid_lo = at("hid_hi", [P, 2, CH], F32R, k3 + 8192), at("hid_lo", [P, 2, CH], F32R, k3 + 12288)
        xh1 = at("xh1", [P, TPC, D], F32, qp_reg + 14336)
        ceT = at("ceT", [3 * CR, T], BF16, qp_reg + 18432)
        h32 = [at("h32a", [P, CH], F32, qp_reg + 22528), at("h32b", [P, CH], F32, k1 + W_B)]
        small = [k0 + W_B]

        def little(name, shape, dt=F32):
            n = int(np.prod(shape[1:])) * (2 if dt == BF16 else 4)
            n = -(-n // 32) * 32
            small[0] += n
            assert small[0] <= k1
            return at(name, shape, dt, small[0] - n)

        lg, pr, rank, ce = (little(n, [P, TPC, E]) for n in ("lg", "pr", "rank", "ce"))
        r4, r4b, tri = little("r4", [P, TPC]), little("r4b", [P, TPC]), little("tri", [P, E, E])
        ce3 = little("ce3", [P, TPC, 3, CR], BF16)
        ident_bf = little("ident_bf", [P, P], BF16)
        cmp1 = at("cmp1", [P, TPC, E, E], F32, k2 + NI * D * 4)
        cmp2 = at("cmp2", [P, TPC, E, E], F32, k2 + NI * D * 4 + 1024)
        wmod1_sb = at("wmod1_sb", [P, KT, 6 * D], F32, p_reg)
        mrow1 = at("mrow1", [P, 6, D], F32, p_reg + 12288)
        cb1 = at("cb1", [P, KT, P], F32, p_reg + 18432)
        xt1 = at("xt1", [P, D], F32, p_reg + 18432)
        rows1 = at("rows1", [P, 5, D], F32, p_reg + 19456)
        RGA = 4
        sdb_row, b1_row = at("sdb_row", [P, D], F32, p_reg), at("b1_row", [P, D], F32, p_reg + 1024)
        yt2 = at("yt2", [P, 2, D], F32, p_reg)
        gsd = at("gsd", [P, D], F32, p_reg + 2048)
        gb1 = at("gb1", [P, D], F32, p_reg + 3072)
        w1_sb = at("w1_sb", [P, KT, D], F32, p_reg + 4096)
        bw = at("bw", [P, KT, D], F32, p_reg + 6144)
        bwT = at("bwT", [P, KT, D], F32, p_reg + 8192)
        att = at("att", [P, KT, D], F32, p_reg + 10240)
        alpha = new("alpha", [P, KT])
        ux, uu = at("ux", [DX, D], F32, k1 + W_B), at("uu", [DX, D], F32, k1 + W_B + 1024)
        ww, xa = at("ww", [DX, D], F32, k2 + NI * D * 4), at("xa", [DX, D], F32, k2 + NI * D * 4 + 1024)

        ps = ctx.enter_context(nc.psum_tensor("ps", [P, 8, CH], F32))

        names = {}

        def sem(name):
            names[name] = ctx.enter_context(nc.semaphore(name))
            return names[name]

        x_in_s = [sem(f"x_loaded{c}") for c in range(NC)]
        mod_in, wqk_in, wv_in, small_in = sem("mod_in"), sem("wqk_in"), sem("wv_in"), sem("small_in")
        consts, bias0 = sem("consts"), sem("bias0")
        c_ready, cb_ready, mcol_ps, mrow_ps = sem("c_ready"), sem("cb_ready"), sem("mcol_ps"), sem("mrow_ps")
        mcol_ready, mrow_ready, rows_step = sem("mcol_ready"), sem("mrow_ready"), sem("rows_step")
        bn_s, var_s, veps_s, rs_s, xh_s = sem("bn_s"), sem("var_s"), sem("veps_s"), sem("rs_s"), sem("xh_s")
        tr_ps, hT_s = sem("tr_ps"), sem("hT_s")
        proj_ps, q32_s, hi_s, r_s, mid_s, split_s = (sem("proj_ps"), sem("q32_s"), sem("hi_s"), sem("r_s"),
                                                     sem("mid_s"), sem("split_s"))
        v_ps, v_s, vconst = sem("v_ps"), sem("v_s"), sem("vconst")
        kst_in = [sem(f"kst_in{g}") for g in range(3)]
        kd_out, qd_out = sem("kd_out"), sem("qd_out")
        kst_one, q_in, nm_in = sem("kst_one"), sem("q_in"), sem("nm_in")
        mx_ps, mx_read, nmx_s = sem("mx_ps"), sem("mx_read"), sem("nmx_s")
        nmT_ps, nmT_s, nm_step, nm_s = sem("nmT_ps"), sem("nmT_s"), sem("nm_step"), sem("nm_s")
        sc_ps, p_s, pv_s, o_s, oT_ps, oT_s = sem("sc_ps"), sem("p_s"), sem("pv_s"), sem("o_s"), sem("oT_ps"), sem("oT_s")
        rec_s, att_step, att_s = sem("rec_s"), sem("att_step"), sem("att_s")
        res_step, res_s = sem("res_step"), sem("res_s")
        ffw_in = [sem(f"ffw_in{n}") for n in range(3)]
        l1_in, mod1_in = sem("l1_in"), sem("mod1_in")
        bn_go = sem("bn_go")
        wg_s, wu_hi_s, wu_s, wd_hi_s, wd_s = sem("wg_s"), sem("wu_hi_s"), sem("wu_s"), sem("wd_hi_s"), sem("wd_s")
        rw_s, wd2_s = sem("rw_s"), sem("wd2_s")
        h_hi_s, h_full_s, h_lo_s = sem("h_hi_s"), sem("h_full_s"), sem("h_lo_s")
        lg_ps, rt, ce_ps, ceT_s, sel_s = sem("lg_ps"), sem("rt"), sem("ce_ps"), sem("ceT_s"), sem("sel_s")
        lg_s, exp_s, ce_s = sem("lg_s"), sem("exp_s"), sem("ce_s")
        g_ps, u_ps, sig_s, t_s, cb_ps, full_s = (sem("g_ps"), sem("u_ps"), sem("sig_s"), sem("t_s"), sem("cb_ps"),
                                                 sem("full_s"))
        hid_hi_s, hid_lo_s, hid_used = sem("hid_hi_s"), sem("hid_lo_s"), sem("hid_used")
        y_read, y_s, xsd_s = sem("y_read"), sem("y_s"), sem("xsd_s")
        row_ps, row_s, rows1_s, gb1_s = sem("row_ps"), sem("row_s"), sem("rows1_s"), sem("gb1_s")
        ux_s, uw_ps, uw_s, s1_ps, relu_s, att_z = (sem("ux_s"), sem("uw_ps"), sem("uw_s"), sem("s1_ps"),
                                                   sem("relu_s"), sem("att_z"))
        hc_s, za_ps, za_read, za_s, xa_s = sem("hc_s"), sem("za_ps"), sem("za_read"), sem("za_s"), sem("xa_s")
        axa_ps, axa_s = sem("axa_ps"), sem("axa_s")
        bw_s, bwT_ps, bwT_s, f_ps, f_read, f_s = (sem("bw_s"), sem("bwT_ps"), sem("bwT_s"), sem("f_ps"),
                                                  sem("f_read"), sem("f_s"))
        res1_s, res1_step, xb_s, out_s = sem("res1_s"), sem("res1_step"), sem("xb_s"), sem("out_s")

        block = ctx.enter_context(nc.Block())
        kd = nc.dram_tensor("k_parts", (3, D, T), BF16, kind="Internal").ap()
        qd = nc.dram_tensor("q_parts", (3, D, T), BF16, kind="Internal").ap()
        x_v = x_in.rearrange("(t p) d -> p t d", p=P)
        out_v = out.rearrange("(t p) d -> p t d", p=P)

        def ln(n, c):
            return NC * n + c if n < 2 else NC * 2 + 2 * c + n - 2

        def x_cols(t, n=1):
            return x[:].rearrange("p t d -> p (t d)")[:, bass.ds(t * D, n * D)]

        @block.sync
        def _(sp):
            for c in range(NC):
                sp.dma_start(x[:, TPC * c:TPC * (c + 1), :], x_v[:, TPC * c:TPC * (c + 1), :]).then_inc(x_in_s[c], 16)
            sp.dma_start(wk_sb[:], wk.rearrange("(k p) n -> p k n", p=P)).then_inc(wqk_in, 16)
            sp.dma_start(wq_sb[:], wq.rearrange("(k p) n -> p k n", p=P)).then_inc(wqk_in, 16)
            sp.dma_start(wv_sb[:], wv.rearrange("(k p) n -> p k n", p=P)).then_inc(wv_in, 16)
            sp.dma_start(bv_row[:], bv.unsqueeze(0).to_broadcast([P, D])).then_inc(wv_in, 16)

            def store_parts(src, dst, ft, c, sem_):
                cols = slice(CH * c, CH * (c + 1))
                sp.dma_start(dst[:, P * ft:P * (ft + 1), cols].rearrange("a p n -> p a n"),
                             src[:, ft, :, cols]).then_inc(sem_, 16)

            def load_k(g, sem_):
                for b in range(BLK):
                    sp.dma_start(kst[DH * b:DH * (b + 1), G * g:G * (g + 1), :],
                                 kd[K_PART[b]].rearrange("(h d) n -> d h n", d=DH)[:, G * g:G * (g + 1), :]
                                 ).then_inc(sem_, 16)

            def load_q(g, c):
                for b in range(BLK):
                    sp.dma_start(qst[DH * b:DH * (b + 1), g, :, :],
                                 qd[Q_PART[b]].rearrange("(h d) n -> d h n", d=DH)[:, G * g:G * (g + 1), bass.ts(c, CH)]
                                 ).then_inc(q_in, 16)

            def store_max(slot):
                for m in range(NM):
                    sp.dma_start(qst[KR + m:KR + m + 1, slot, :, :].rearrange("p k (j n) -> p (k j) n", j=TPC),
                                 nmp[:, m, :]).then_inc(nm_in, 16)

            def load_gate_up(dst, experts, shared, sem_):
                for k in range(KT):
                    sp.dma_start(dst[:, :, 0:E * I].rearrange("p k (e i) -> p k e i", e=E)[:, k],
                                 experts.rearrange("e (k p) i -> k p e i", p=P)[k]).then_inc(sem_, 16)
                sp.dma_start(dst[:, :, E * I:IA], shared.rearrange("(k p) i -> p k i", p=P)).then_inc(sem_, 16)

            for c in range(NC):
                for ft in range(KT):
                    sp.wait_ge(split_s, KT * c + ft + 1)
                    store_parts(kp, kd, ft, c, kd_out)
            sp.wait_ge(kd_out, 16 * KT * NC)
            load_k(0, kst_in[0])
            for c in range(NC):
                for ft in range(KT):
                    sp.wait_ge(split_s, KT * NC + KT * c + ft + 1)
                    store_parts(qp, qd, ft, c, qd_out)
                if c == 0:
                    sp.wait_ge(qd_out, 16 * KT)
                    load_q(0, 0)
                    load_k(1, kst_in[1])
                    sp.wait_ge(q_in, 16 * BLK)
                    load_q(1, 0)
                    sp.wait_ge(q_in, 16 * BLK * 2)
            load_k(2, kst_in[2])
            load_k(3, kst_in[2])
            sp.wait_ge(qd_out, 16 * KT * NC)
            sp.wait_ge(nm_s, 1)
            store_max(0)
            sp.wait_ge(nm_in, 16 * NM)
            for v in range(2, G):
                load_q(v, 0)
                sp.wait_ge(q_in, 16 * BLK * (v + 1))
                sp.wait_ge(nm_s, v)
                store_max(v - 1)
                sp.wait_ge(nm_in, 16 * NM * v)
            for v in range(G, NU):
                c, g = v // NG, v % NG
                sp.wait_ge(sc_ps, G * MT * (v - NG + 1))
                load_q(g, c)
                sp.wait_ge(q_in, 16 * BLK * (v + 1))
                sp.wait_ge(nm_s, v)
                store_max((v - 1) % NG)
                sp.wait_ge(nm_in, 16 * NM * v)
                if v == G:
                    load_gate_up(wg_raw, gate_w, sg_w, ffw_in[0])
            sp.wait_ge(nm_s, NU)
            store_max(NG - 1)
            sp.wait_ge(sc_ps, G * MT * (NU - 2))
            load_gate_up(wu_raw, up_w, su_w, ffw_in[1])
            sp.wait_ge(sc_ps, G * MT * (NU - 1))
            sp.dma_start(wd_raw[:, 0:IE, :], down_w.rearrange("e i d -> (e i) d").rearrange("(t p) d -> p t d", p=P)
                         ).then_inc(ffw_in[2], 16)
            sp.dma_start(wd_raw[:, IE:NI - 1, :], sd_w[0:(NI - 1 - IE) * P, :].rearrange("(t p) d -> p t d", p=P)
                         ).then_inc(ffw_in[2], 16)
            sp.dma_start(wd_raw[0:LAST, NI - 1, :], sd_w[(NI - 1 - IE) * P:SI, :]).then_inc(ffw_in[2], 16)
            sp.wait_ge(pv_s, MT * NU)
            sp.dma_start(wmod1_sb[:], wmod1.rearrange("(k p) n -> p k n", p=P)).then_inc(mod1_in, 16)
            sp.wait_ge(row_ps, 3)
            sp.wait_ge(mcol_ps, 2)
            sp.dma_start(sdb_row[:], sd_b.unsqueeze(0).to_broadcast([P, D])).then_inc(l1_in, 16)
            sp.dma_start(b1_row[:], b1.unsqueeze(0).to_broadcast([P, D])).then_inc(l1_in, 16)
            sp.dma_start(w1_sb[:], w1.rearrange("(k p) n -> p k n", p=P)).then_inc(l1_in, 16)
            for c in range(NC):
                sp.wait_ge(f_s, 2 * (c + 1))
                sp.dma_start(out_v[:, TPC * c:TPC * (c + 1), :], x[:, TPC * c:TPC * (c + 1), :]).then_inc(out_s, 16)
            sp.wait_ge(out_s, 16 * NC)

        @block.tensor
        def _(pe):
            def mod_columns(n, wmod_n, bank):
                for j in range(12):
                    for k in range(KT):
                        last = nc.tensor.matmul(ps[:, bank, j:j + 1], wmod_n[:, k, P * j:P * (j + 1)],
                                                c_sil[n][:, k:k + 1], start=k == 0, stop=k == KT - 1)
                last.then_inc(mcol_ps, 1)

            def mod_row(wmod_n, cb_n, j, bank):
                for k in range(KT):
                    last = nc.tensor.matmul(ps[:, bank, :], cb_n[:, k, :], wmod_n[:, k, CH * j:CH * (j + 1)],
                                            start=k == 0, stop=k == KT - 1)
                return last

            def transposes(n, c):
                q = ln(n, c)
                pe.wait_ge(xh_s, TPC * (q + 1))
                pe.wait_ge(hT_s, KT * q)
                for ft in range(KT):
                    for j in range(TPC):
                        last = nc.tensor.transpose(ps[:, ft, P * j:P * (j + 1)],
                                                   xh[:, q % 2, j, P * ft:P * (ft + 1)], ident[:])
                    last.then_inc(tr_ps, 1)

            def project(i, w, c, ft):
                pe.wait_ge(hT_s, KT * (c + 1))
                if i >= 2:
                    pe.wait_ge(q32_s, i - 1)
                for k in range(KT):
                    last = nc.tensor.matmul(ps[:, 2 + i % 2, :], w[:, k, P * ft:P * (ft + 1)],
                                            hT[:, k, CH * c:CH * (c + 1)], start=k == 0, stop=k == KT - 1)
                last.then_inc(proj_ps, 1)

            pe.wait_ge(mod_in, 32)
            pe.wait_ge(c_ready, 1)
            pe.wait_ge(cb_ready, 1)
            mod_columns(0, wmod_sb, 7)
            for j in range(3):
                last = mod_row(wmod_sb, cb, j, 4 + j)
            last.then_inc(mrow_ps, 1)
            pe.wait_ge(consts, 1)
            transposes(0, 0)
            pe.wait_ge(wqk_in, 32)
            for c in range(1, NC):
                transposes(0, c)
                for ft in range(KT):
                    project(KT * (c - 1) + ft, wk_sb, c - 1, ft)
            for ft in range(KT):
                project(KT * (NC - 1) + ft, wk_sb, NC - 1, ft)
            for c in range(NC):
                for ft in range(KT):
                    project(KT * NC + KT * c + ft, wq_sb, c, ft)
            pe.wait_ge(wv_in, 32)
            for i in range(MT // 2):
                if i < 2:
                    pe.wait_ge(mrow_ready, 1)
                else:
                    pe.wait_ge(v_s, i - 1)
                for j in range(2):
                    for k in range(KT):
                        last = nc.tensor.matmul(ps[:, 4 + i % 2, D * j:D * (j + 1)],
                                                hT[:, k, P * (2 * i + j):P * (2 * i + j + 1)], wv_sb[:, k, :],
                                                start=k == 0, stop=k == KT - 1)
                last.then_inc(v_ps, 1)

            def maxima(g, i, p, n):
                if not isinstance(n, int) or n >= 2:
                    pe.wait_ge(mx_read, n - 1)
                hd, j = i // TPC, i % TPC
                for m in range(2):
                    col = CH * (2 * p + m)
                    last = nc.tensor.matmul(ps[:, 2 * p + m, :], qst[0:KR, g, hd, P * j:P * (j + 1)],
                                            kst[0:KR, G * g + hd, col:col + CH], start=True, stop=True)
                last.then_inc(mx_ps, 1)

            def max_row(v, n_pairs):
                pe.wait_ge(nmx_s, v + 1)
                pe.wait_ge(mx_read, n_pairs)
                nc.tensor.transpose(ps[0:MI, 2, 0:P], nmx[:], ident[:]).then_inc(nmT_ps, 1)

            def unit(u, g, ahead, first=False, extra={}):
                pe.wait_ge(nm_in, (u + 1) * (16 * NM))
                for t in range(MT):
                    run = (t + LEAD < MI and ahead >= 1) or (t + LEAD >= MI and ahead >= 2)
                    nxt = t + LEAD < MI
                    i = (t + LEAD) % MI
                    v, vg = (u + 1, (g + 1) % NG) if nxt else (u + 2, (g + 2) % NG)
                    if run and i == 0:
                        pe.wait_ge(q_in, (u + 3) * (16 * BLK))
                    pairs = v * (2 * MI) + 2 * i
                    if run:
                        if t == 4 and not first:
                            pe.wait_ge(oT_s, u)
                        maxima(vg, i, 0, pairs)
                    for k in range(G):
                        if k == 0 and not (first and t == 0):
                            pe.wait_ge(p_s, u * (G * MT) + G * t)
                        if k == G - 1:
                            pe.wait_ge(p_s, u * (G * MT) + G * t + 1)
                        if k == 2 and run:
                            if t == 14:
                                pe.wait_ge(nmT_s, u + 2)
                            maxima(vg, i, 1, pairs + 1)
                        nc.tensor.matmul(ps[:, 4 + k % 3, :], kst[0:KR + NM, G * g + k, P * t:P * (t + 1)],
                                         qst[0:KR + NM, g, k, :], start=True, stop=True).then_inc(sc_ps, 1)
                    if t == 3 and not first:
                        pe.wait_ge(o_s, u)
                        if ahead >= 1:
                            pe.wait_ge(mx_read, pairs + 1)
                        for j in range(TPC):
                            last = nc.tensor.transpose(ps[:, 0, P * j:P * (j + 1)], o_sb[:, P * j:P * (j + 1)], ident[:])
                        last.then_inc(oT_ps, 1)
                    if t == 13 and ahead >= 1:
                        max_row(u + 1, (u + 2) * (2 * MI) + (4 if ahead >= 2 else 0))
                    if t == 0 and not first:
                        weigh((g - 1) % NG, MT - 1)
                    if t >= 1:
                        if t == 1 and not first:
                            pe.wait_ge(o_s, u)
                        weigh(g, t - 1)
                    for work in extra.get(t, ()):
                        work()

            def weigh(g, t):
                for k in range(G):
                    last = nc.tensor.matmul(ps[VW * k:VW * (k + 1), 7, :], vp[:, t, G * g + k, :], prob[:, t % 2, k, :],
                                            start=t == 0, stop=t == MT - 1)
                last.then_inc(pv_s, 1)

            pe.wait_ge(kst_in[0], 16 * BLK)
            pe.wait_ge(q_in, 16 * BLK)
            pe.wait_ge(q32_s, 2 * KT * NC)
            for i in range(MI):
                for p in range(2):
                    maxima(0, i, p, 2 * i + p)
            max_row(0, 2 * MI)
            pe.wait_ge(kst_in[1], 16 * BLK)
            pe.wait_ge(q_in, 16 * BLK * 2)
            for i in range(LEAD):
                for p in range(2):
                    if i == 0 and p == 1:
                        pe.wait_ge(nmT_s, 1)
                    maxima(1, i, p, 2 * MI + 2 * i + p)
            pe.wait_ge(v_s, MT // 2)
            pe.wait_ge(vconst, 1)
            pe.wait_ge(kst_one, 1)
            pe.wait_ge(kst_in[2], 32 * BLK)
            unit(0, 0, 2, first=True)
            with pe.Fori(0, NC - 1) as c:
                for g in range(1, NG + 1):
                    unit(c * NG + g, g % NG, 2)
            def turn(q, ft, bank):
                pe.wait_ge(xh_s, TPC * (q + 1))
                for j in range(TPC):
                    last = nc.tensor.transpose(ps[:, bank, P * j:P * (j + 1)], xh1[:, j, P * ft:P * (ft + 1)], ident[:])
                last.then_inc(tr_ps, 1)

            def turn_both(c):
                if c:
                    pe.wait_ge(h_full_s, KT * c)
                for ft in range(KT):
                    turn(ln(1, c), ft, 1 + ft)

            def hT_pair(part, k, c):
                return (hT_hi[:, k, bass.ts(c, CH)], hT_lo[:, bass.ds((c * KT + k) * CH, CH)])[part]

            def logits(c, bank, col):
                pe.wait_ge(h_lo_s, KT * (c + 1))
                pe.wait_ge(rw_s, 2)
                for j in range(TPC):
                    n = 0
                    for k in range(KT):
                        lo_at = (c * KT + k) * CH + P * j
                        for a, b in ((hT_hi[:, k, CH * c + P * j:CH * c + P * (j + 1)], rw_hi),
                                     (hT_hi[:, k, CH * c + P * j:CH * c + P * (j + 1)], rw_lo),
                                     (hT_lo[:, lo_at:lo_at + P], rw_hi)):
                            last = nc.tensor.matmul(ps[:, bank, col + E * j:col + E * (j + 1)], a, b[:, k, :],
                                                    start=n == 0, stop=n == 3 * KT - 1)
                            n += 1
                last.then_inc(lg_ps, 1)

            def turn_combine(c, bank):
                pe.wait_ge(ce_s, c + 1)
                for j in range(TPC):
                    last = nc.tensor.matmul(ps[0:3 * CR, bank, P * j:P * (j + 1)],
                                            ce3[:, j, :, :].rearrange("p a e -> p (a e)"), ident_bf[:], start=True, stop=True)
                last.then_inc(ce_ps, 1)

            def combine_in_bank0(c):
                pe.wait_ge(oT_s, NU - 1)
                if c:
                    pe.wait_ge(ceT_s, c)
                turn_combine(c, 0)

            for g in range(1, NG - 1):
                unit(NU - NG + g, g, min(2, NG - 1 - g))
            unit(NU - 1, NG - 1, 0, extra={
                0: [lambda: turn_both(0)], 4: [lambda: logits(0, 3, 0)], 6: [lambda: turn_both(1)],
                8: [lambda: combine_in_bank0(0), lambda: logits(1, 3, 32)], 10: [lambda: turn_both(2)],
                12: [lambda: combine_in_bank0(1), lambda: logits(2, 3, 64)], 15: [lambda: combine_in_bank0(2)]})
            pe.wait_ge(p_s, NU * G * MT)
            weigh(NG - 1, MT - 1)
            pe.wait_ge(o_s, NU)
            pe.wait_ge(ceT_s, NC - 1)
            for j in range(TPC):
                last = nc.tensor.transpose(ps[:, 0, P * j:P * (j + 1)], o_sb[:, P * j:P * (j + 1)], ident[:])
            last.then_inc(oT_ps, 1)

            PASSES = ((0, 0), (0, 1), (1, 0))

            def down(n, it, c_read):
                rows = P if it < NI - 1 else LAST
                if c_read is not None:
                    pe.wait_ge(y_read, c_read)
                for part, (a, b) in enumerate(((hid_hi, wd_hi), (hid_hi, wd_lo), (hid_lo, wd_hi))):
                    if part == 0:
                        pe.wait_ge(hid_hi_s, n + 1)
                    if part == 2:
                        pe.wait_ge(hid_lo_s, n + 1)
                    for j in range(TPC):
                        last = nc.tensor.matmul(ps[:, 6 + j // 2, D * (j % 2):D * (j % 2 + 1)],
                                                a[0:rows, it % 2, P * j:P * (j + 1)], b[0:rows, it, :],
                                                start=it == 0 and part == 0 and j % 2 == 0,
                                                stop=it == NI - 1 and part == 2, skip_group_check=True)
                last.then_inc(hid_used, 1)

            def chunk(c, slots, first=False):
                for it in range(NI):
                    rows = P if it < NI - 1 else LAST
                    n = c * NI + it
                    if first and it == 0:
                        pe.wait_ge(wg_s, 2 * KT)
                        pe.wait_ge(oT_s, NU)
                    if first and it in (0, EARLY):
                        pe.wait_ge(wu_s, 1 if it == 0 else 2)
                    if first and it in (1, EARLY + 1):
                        pe.wait_ge(wd_s, 1)
                    if first and it == EARLY + 1:
                        pe.wait_ge(wd2_s, 4)
                    if not (first and it < 2):
                        pe.wait_ge(t_s, n - 1)
                    for w, b, done in (((wg_hi, wg_lo), 0, g_ps), ((wu_hi, wu_lo), 2, u_ps)):
                        m = 0
                        for k in range(KT):
                            for wp, hp in PASSES:
                                last = nc.tensor.matmul(ps[0:rows, b + it % 2, :], w[wp][:, k, P * it:P * it + rows],
                                                        hT_pair(hp, k, c), start=m == 0, stop=m == 3 * KT - 1)
                                m += 1
                        last.then_inc(done, 1)
                    if it < IE:
                        if first and it == 0:
                            pe.wait_ge(ceT_s, NC - 1)
                            pe.wait_ge(sel_s, 1)
                        else:
                            pe.wait_ge(full_s, c * IE + it)
                        nc.tensor.matmul(ps[:, 4, :], sel[:, P * it:P * (it + 1)], ceT[:, bass.ts(c, CH)],
                                         start=True, stop=True).then_inc(cb_ps, 1)
                    for work in slots.get(it, ()):
                        work(c)
                    if it >= 1:
                        down(n - 1, it - 1, c if it == 1 and not first else None)
                    elif not first:
                        down(n - 1, NI - 1, None)

            def turn3(ft):
                def work(c):
                    if ft == 1:
                        pe.wait_ge(h_full_s, KT * (NC - 1) + 1)
                    turn(ln(1, NC - 1), ft, 5)
                return work

            def logits3(c):
                pe.wait_ge(h_full_s, KT * NC)
                logits(NC - 1, 5, 0)

            def combine3(c):
                pe.wait_ge(lg_s, NC)
                turn_combine(NC - 1, 5)

            def columns1(c):
                pe.wait_ge(ceT_s, NC)
                pe.wait_ge(mod1_in, 16)
                mod_columns(1, wmod1_sb, 5)

            def row1(j):
                def work(c):
                    if j == 0:
                        pe.wait_ge(cb_ready, 2)
                        pe.wait_ge(mcol_ready, 2)
                    else:
                        pe.wait_ge(row_s, j)
                    mod_row(wmod1_sb, cb1, j, 5).then_inc(row_ps, 1)
                return work

            chunk(0, {5: [turn3(0)], 6: [turn3(1)], 7: [logits3], 8: [combine3], 9: [columns1],
                      10: [row1(0)], 11: [row1(1)], 12: [row1(2)]}, first=True)

            def l1_turn(n, ft):
                def work(c):
                    d = c - 1
                    if n == 2 and ft == 0:
                        if isinstance(c, int) and c == 1:
                            pe.wait_ge(row_s, 3)
                        else:
                            pe.wait_ge(f_read, 2 * d)
                    elif ft == 0:
                        pe.wait_ge(za_read, 2 * d + 2)
                        if isinstance(c, int) and c == 1:
                            pe.wait_ge(bwT_s, 1)
                    else:
                        pe.wait_ge(hc_s, 4 * d + 2 * (n - 2) + 1)
                    turn(ln(n, d), ft, 5)
                return work

            def l1_uw(c):
                pe.wait_ge(ux_s, 1)
                pe.wait_ge(hc_s, 2)
                for n, w in enumerate((BT_sb, CT_sb)):
                    last = nc.tensor.matmul(ps[0:DX, 5, D * n:D * (n + 1)], w[:], ux[:], start=True, stop=True)
                last.then_inc(uw_ps, 1)

            def l1_scores(c):
                pe.wait_ge(uw_s, 1)
                for n in range(KT):
                    last = nc.tensor.matmul(ps[:, 5, D * n:D * (n + 1)], uu[:, P * n:P * (n + 1)], ww[:], start=True, stop=True)
                last.then_inc(s1_ps, 1)

            def l1_attend(half):
                def work(c):
                    d = c - 1
                    if half == 0:
                        pe.wait_ge(hc_s, 4 * d + 2)
                        pe.wait_ge(att_z, 1)
                    else:
                        pe.wait_ge(za_read, 2 * d + 1)
                        pe.wait_ge(axa_s, 1)
                    for i in range(2):
                        j = 2 * half + i
                        for k in range(KT):
                            last = nc.tensor.matmul(ps[:, 5, D * i:D * (i + 1)], hTc[:, k, P * j:P * (j + 1)], att[:, k, :],
                                                    start=k == 0, stop=k == KT - 1)
                    last.then_inc(za_ps, 1)
                return work

            def l1_a(c):
                pe.wait_ge(xa_s, 1)
                pe.wait_ge(za_read, 1)
                nc.tensor.matmul(ps[0:DX, 5, 0:D], AT_sb[:], xa[:], start=True, stop=True).then_inc(axa_ps, 1)

            def l1_weights(c):
                pe.wait_ge(bw_s, 1)
                pe.wait_ge(za_read, 2)
                for k in range(KT):
                    for o in range(KT):
                        last = nc.tensor.transpose(ps[:, 5, P * (KT * k + o):P * (KT * k + o + 1)],
                                                   bw[:, o, P * k:P * (k + 1)], ident[:])
                last.then_inc(bwT_ps, 1)

            def l1_feed(half):
                def work(c):
                    d = c - 1
                    if half == 0:
                        pe.wait_ge(hc_s, 4 * d + 4)
                    else:
                        pe.wait_ge(f_read, 2 * d + 1)
                    for i in range(2):
                        j = 2 * half + i
                        for k in range(KT):
                            last = nc.tensor.matmul(ps[:, 5, D * i:D * (i + 1)], hTc[:, k, P * j:P * (j + 1)], bwT[:, k, :],
                                                    start=k == 0, stop=k == KT - 1)
                    last.then_inc(f_ps, 1)
                return work

            rest = {2: [l1_turn(2, 0)], 3: [l1_turn(2, 1)], 6: [l1_attend(0)], 8: [l1_attend(1)],
                    10: [l1_turn(3, 0)], 11: [l1_turn(3, 1)], 12: [l1_feed(0)], 13: [l1_feed(1)]}
            chunk(1, {**rest, 4: [l1_uw], 5: [l1_scores], 7: [l1_a], 9: [l1_weights]})
            with pe.Fori(2, NC) as c:
                chunk(c, rest)
            down(NC * NI - 1, NI - 1, None)
            for it in sorted(rest):
                for work in rest[it]:
                    work(NC)

        @block.scalar
        def _(act):
            act.dma_start(c_col[0][:], c0.rearrange("o (k p) -> p (o k)", p=P), allow_slow_non_contiguous=True).then_inc(mod_in, 16)
            act.dma_start(wmod_sb[:], wmod0.rearrange("(k p) n -> p k n", p=P)).then_inc(mod_in, 16)
            small = [(bk_col[:], bk.rearrange("(k p) -> p k", p=P)), (bq_col[:], bq.rearrange("(k p) -> p k", p=P)),
                     (c_col[1][:], c1.rearrange("o (k p) -> p (o k)", p=P)),
                     (rw[:], routerT.rearrange("(k p) e -> p k e", p=P)),
                     (AT_sb[:], AT), (BT_sb[:], BT), (CT_sb[:], CT), (r_col[:], r_l.unsqueeze(0).to_broadcast([P, 1]))]
            for dst, src in small:
                act.dma_start(dst, src, allow_slow_non_contiguous=True).then_inc(small_in, 16)
            act.wait_ge(bias0, 1)
            n_small = len(small)
            for b_sb, b in ((bg, sg_b), (bu, su_b)):
                act.dma_start(b_sb[:, IE:NI - 1], b[0:(NI - 1 - IE) * P].rearrange("(t p) -> p t", p=P),
                              allow_slow_non_contiguous=True).then_inc(small_in, 16)
                act.dma_start(b_sb[0:LAST, NI - 1:NI], b[(NI - 1 - IE) * P:SI].unsqueeze(1)).then_inc(small_in, 16)
            act.wait_ge(mod_in, 32)
            act.wait_ge(small_in, 16 * (n_small + 4))
            for n in range(2):
                last = nc.scalar.activation(c_sil[n][:], c_col[n][:], ACT.Silu)
            last.then_inc(c_ready, 1)
            act.wait_ge(consts, 1)

            def modulate(n, c):
                q = ln(n, c)
                for ft in range(KT):
                    act.wait_ge(tr_ps, KT * q + ft + 1)
                    nc.scalar.activation(hT[:, ft, CH * c:CH * (c + 1)], ps[:, ft, :], ACT.Identity,
                                         scale=mcol[0][:, 2 + ft:3 + ft],
                                         bias=mcol[0][:, ft:1 + ft]).then_inc(hT_s, 1)

            def proj(i, b_col, ft):
                act.wait_ge(proj_ps, i + 1)
                if i >= 2:
                    act.wait_ge(split_s, i - 1)
                nc.scalar.activation(q32[:, i % 2, :], ps[:, 2 + i % 2, :], ACT.Identity,
                                     bias=b_col[:, ft:ft + 1]).then_inc(q32_s, 1)

            act.wait_ge(mcol_ready, 1)
            modulate(0, 0)
            for c in range(1, NC):
                modulate(0, c)
                for ft in range(KT):
                    proj(KT * (c - 1) + ft, bk_col, ft)
            for ft in range(KT):
                proj(KT * (NC - 1) + ft, bk_col, ft)
            for c in range(NC):
                for ft in range(KT):
                    proj(KT * NC + KT * c + ft, bq_col, ft)

            def max_rows(v):
                act.wait_ge(nmT_ps, v + 1)
                act.wait_ge(nm_s, v)
                nc.scalar.activation(nm32[:], ps[0:MI, 2, 0:P], ACT.Copy).then_inc(nmT_s, 1)

            def leave_output(u):
                act.wait_ge(pv_s, (u + 1) * MT)
                nc.scalar.activation(o_sb[:], ps[:, 7, :], ACT.Copy).then_inc(o_s, 1)

            def leave_transposed(u):
                act.wait_ge(oT_ps, u + 1)
                if isinstance(u, int) and u == NU - 1:
                    act.wait_ge(att_s, u)
                else:
                    act.wait_ge(nm_s, u + 2)
                nc.scalar.activation(o_tm[:].rearrange("p j k w -> p (j k w)"), ps[:, 0, :], ACT.Copy).then_inc(oT_s, 1)

            def router_exp(c):
                act.wait_ge(lg_s, c + 1)
                nc.scalar.activation(pr[:], lg[:], ACT.Exp).then_inc(exp_s, 1)

            def unit(u, first, ahead, extra={}):
                for t in range(MT):
                    if t in extra:
                        router_exp(extra[t])
                    if t == 1 and not first:
                        leave_output(u - 1)
                    if t == 4 and not first:
                        leave_transposed(u - 1)
                    if t == 14 and ahead >= 1:
                        max_rows(u + 1)
                    for k in range(G):
                        act.wait_ge(sc_ps, u * (G * MT) + G * t + k + 1)
                        if k == 0 and not (first and t < 2):
                            act.wait_ge(pv_s, u * MT + t - 1)
                        nc.scalar.activation(prob[:, t % 2, k, :], ps[:, 4 + k % 3, :], ACT.Exp,
                                             scale=DH ** -0.5).then_inc(p_s, 1)

            max_rows(0)
            act.wait_ge(kd_out, 16 * KT * NC)
            unit(0, True, 2)
            with act.Fori(1, NU - 2) as u:
                unit(u, False, 2)
            unit(NU - 2, False, 1)
            unit(NU - 1, False, 0, extra={7: 0, 11: 1, 15: 2})
            leave_output(NU - 1)

            early, late = slice(0, P * EARLY), slice(P * EARLY, IA)
            act.wait_ge(ffw_in[1], 48)
            nc.scalar.activation(wu_hi[:, :, early], wu_raw[:, :, early], ACT.Copy).then_inc(wu_hi_s, 1)
            leave_transposed(NU - 1)
            nc.scalar.activation(wu_hi[:, :, late], wu_raw[:, :, late], ACT.Copy).then_inc(wu_hi_s, 1)
            act.wait_ge(ffw_in[2], 48)
            nc.scalar.activation(wd_hi[:, 0:EARLY, :], wd_raw[:, 0:EARLY, :], ACT.Copy).then_inc(wd_hi_s, 1)

            def chunk(c, slots, first=False):
                for it in range(NI):
                    rows = P if it < NI - 1 else LAST
                    n = c * NI + it
                    act.wait_ge(g_ps, n + 1)
                    if not (first and it < 2):
                        act.wait_ge(t_s, n - 1)
                    nc.scalar.activation(sig[0:rows, it % 2, :], ps[0:rows, it % 2, :], ACT.Silu,
                                         bias=bg[0:rows, it:it + 1]).then_inc(sig_s, 1)
                    if it < IE:
                        act.wait_ge(full_s, c * IE + it + 1)
                    else:
                        act.wait_ge(t_s, n + 1)
                    if not (first and it < 2):
                        act.wait_ge(hid_used, n - 1)
                    nc.scalar.activation(hid_hi[0:rows, it % 2, :], hid[0:rows, it % 2, :], ACT.Copy).then_inc(hid_hi_s, 1)
                    for work in slots.get(it, ()):
                        work(c)

            def l1_modulate(n, ft):
                def work(c):
                    col = 0 if n == 2 else 6
                    act.wait_ge(tr_ps, KT * ln(n, c - 1) + ft + 1)
                    nc.scalar.activation(hTc[:, ft, :], ps[:, 5, :], ACT.Identity,
                                         scale=mcol[1][:, col + 2 + ft:col + 3 + ft],
                                         bias=mcol[1][:, col + ft:col + 1 + ft]).then_inc(hc_s, 1)
                return work

            def relu_scores(c):
                act.wait_ge(s1_ps, 1)
                nc.scalar.activation(att[:].rearrange("p k m -> p (k m)"), ps[:, 5, :], ACT.Relu).then_inc(relu_s, 1)

            chunk(0, {7: [lambda c: router_exp(NC - 1)]}, first=True)
            rest = {2: [l1_modulate(2, 0)], 3: [l1_modulate(2, 1)], 10: [l1_modulate(3, 0)], 11: [l1_modulate(3, 1)]}
            chunk(1, {**rest, 5: [relu_scores]})
            with act.Fori(2, NC) as c:
                chunk(c, rest)
            for it in sorted(rest):
                for work in rest[it]:
                    work(NC)

        @block.vector
        def _(dve):
            steps = [0]

            def then(ins):
                steps[0] += 1
                ins.then_inc(rows_step, 1)
                dve.wait_ge(rows_step, steps[0])

            for b_sb in (bg, bu):
                last = nc.vector.memset(b_sb[:], 0.0)
            last.then_inc(bias0, 1)

            def statistics(n, c, complete=None):
                q = ln(n, c)
                mv = mv0[:, TPC * c:TPC * (c + 1), :] if n == 0 else mv1[:]
                if n >= 2:
                    dve.wait_ge(*complete)
                if n or c:
                    dve.wait_ge(var_s, TPC * q)
                if n >= 2:
                    dve.sem_inc(bn_go, 1)
                for j in range(TPC):
                    nc.vector.bn_stats(bn_st[:, j, :], x_cols(c * TPC + j)).then_inc(bn_s, 1)
                dve.wait_ge(bn_s, TPC * (q + 1))
                if n:
                    dve.wait_ge(xh_s, TPC * q)
                if n >= 2:
                    dve.sem_inc(bn_go, 1)
                for j in range(TPC):
                    nc.vector.bn_aggr(mv[:, j, :], bn_st[:, j, :]).then_inc(var_s, 1)

            def normalise(n, c):
                q = ln(n, c)
                dve.wait_ge(rs_s, q + 1)
                if n:
                    dve.wait_ge(tr_ps, KT * q)
                elif c >= 2:
                    dve.wait_ge(tr_ps, KT * (q - 1))
                for j in range(TPC):
                    t = TPC * c + j
                    mean, rs = (mv0[:, t, 0:1], rs0[:, t:t + 1]) if n == 0 else (mv1[:, j, 0:1], rs1[:, j:j + 1])
                    dst = xh[:, q % 2, j, :] if n == 0 else xh1[:, j, :]
                    nc.vector.tensor_scalar(dst, x_cols(t), mean, rs, ALU.subtract, ALU.mult).then_inc(xh_s, 1)

            def broadcast_c(n, cb_n):
                for k in range(KT):
                    last = nc.vector.tensor_copy(cb_n[:, k, :], c_sil[n][:, k:k + 1].to_broadcast([P, P]))
                last.then_inc(cb_ready, 1)

            def columns(n, bank):
                dve.wait_ge(mcol_ps, n + 1)
                then(nc.vector.tensor_copy(mcol[n][:], ps[:, bank, 0:12]))
                for a in (2, 8):
                    last = nc.vector.tensor_scalar(mcol[n][:, a:a + 2], mcol[n][:, a:a + 2], 1.0, None, ALU.add)
                last.then_inc(mcol_ready, 1)

            def gate_row(dst, src, tmp):
                then(nc.vector.tensor_scalar(tmp, src, 0.0, 2.0, ALU.is_ge, ALU.mult))
                then(nc.vector.scalar_tensor_tensor(dst, src, -1.0, src, ALU.mult, ALU.max))
                then(nc.vector.tensor_scalar(dst, dst, 0.25, None, ALU.max))
                then(nc.vector.scalar_tensor_tensor(dst, tmp, -1.0, dst, ALU.add, ALU.mult))

            def modulation_rows(mr, rows):
                gate_row(rows[:, GA, :], mr[:, 2, :], rows[:, GCA, :])
                gate_row(rows[:, GB, :], mr[:, 5, :], rows[:, GCA, :])
                then(nc.vector.scalar_tensor_tensor(rows[:, GCA, :], mr[:, 1, :], 1.0, rows[:, GA, :], ALU.add, ALU.mult))
                return nc.vector.tensor_tensor(rows[:, GSA, :], mr[:, 0, :], rows[:, GA, :], ALU.mult)

            def split(i, parts, ft, c):
                b, cols = i % 2, slice(CH * c, CH * (c + 1))
                dve.wait_ge(q32_s, i + 1)
                nc.vector.tensor_copy(parts[:, ft, 0, cols], q32[:, b, :]).then_inc(hi_s, 1)
                dve.wait_ge(hi_s, i + 1)
                nc.vector.tensor_tensor(res[:, b, :], q32[:, b, :], parts[:, ft, 0, cols], ALU.subtract).then_inc(r_s, 1)
                dve.wait_ge(r_s, i + 1)
                nc.vector.tensor_copy(parts[:, ft, 1, cols], res[:, b, :]).then_inc(mid_s, 1)
                dve.wait_ge(mid_s, i + 1)
                nc.vector.tensor_tensor(parts[:, ft, 2, cols], res[:, b, :], parts[:, ft, 1, cols],
                                        ALU.subtract).then_inc(split_s, 1)

            dve.wait_ge(x_in_s[0], 16)
            statistics(0, 0)
            dve.wait_ge(c_ready, 1)
            broadcast_c(0, cb)
            columns(0, 7)
            normalise(0, 0)
            dve.wait_ge(x_in_s[1], 16)
            statistics(0, 1)
            normalise(0, 1)
            dve.wait_ge(mrow_ps, 1)
            for j in range(3):
                ins = nc.vector.tensor_copy(mrow[:, 2 * j:2 * j + 2, :].rearrange("p a d -> p (a d)"), ps[:, 4 + j, :])
            then(ins)
            modulation_rows(mrow, rows0).then_inc(mrow_ready, 1)
            for c in range(2, NC):
                dve.wait_ge(x_in_s[c], 16)
                statistics(0, c)
                normalise(0, c)
                for ft in range(KT):
                    split(KT * (c - 2) + ft, kp, ft, c - 2)
            for c in range(2, NC):
                for ft in range(KT):
                    split(KT * c + ft, kp, ft, c)
            for c in range(NC):
                for ft in range(KT):
                    split(KT * NC + KT * c + ft, qp, ft, c)
            dve.wait_ge(wv_in, 32)
            dve.wait_ge(vconst, 1)
            for i in range(MT // 2):
                dve.wait_ge(v_ps, i + 1)
                nc.vector.tensor_tensor(vp[:, 2 * i:2 * i + 2, :, 0:DH],
                                        ps[:, 4 + i % 2, :].rearrange("p (j h d) -> p j h d", j=2, h=H),
                                        bv_row[:].rearrange("p (h d) -> p h d", h=H).unsqueeze(1).to_broadcast([P, 2, H, DH]),
                                        ALU.add).then_inc(v_s, 1)

            def reduce_pair(i, p, n):
                dve.wait_ge(mx_ps, n + 1)
                nc.vector.tensor_reduce(mxp[:, i, p:p + 1], ps[:, 2 * p:2 * p + 2, :], AX.XY, ALU.max).then_inc(mx_read, 1)

            def negative_max(v):
                dve.wait_ge(mx_read, (v + 1) * (2 * MI))
                dve.wait_ge(nmT_ps, v)
                nc.vector.tensor_reduce(nmx[:], mxp[:], AX.X, ALU.max, negate=True).then_inc(nmx_s, 1)

            def invert_sums(u):
                dve.wait_ge(oT_s, u + 1)
                nc.vector.reciprocal(rec[:], o_tm[:, :, :, DH]).then_inc(rec_s, 1)

            def unit(u, first, ahead, extra=()):
                for t in range(MT):
                    i = (t + LEAD) % MI
                    v = u + 1 if t + LEAD < MI else u + 2
                    run = (t + LEAD < MI and ahead >= 1) or (t + LEAD >= MI and ahead >= 2)
                    if run:
                        for p in range(2):
                            if i == 0 and p == 0:
                                dve.wait_ge(nmx_s, v)
                            reduce_pair(i, p, v * (2 * MI) + 2 * i + p)
                    if t + LEAD == MI - 1 and ahead >= 1:
                        negative_max(u + 1)
                    if t == 5 and not first:
                        invert_sums(u - 1)

            for i in range(MI):
                for p in range(2):
                    reduce_pair(i, p, 2 * i + p)
            negative_max(0)
            dve.wait_ge(nmx_s, 1)
            for i in range(LEAD):
                for p in range(2):
                    reduce_pair(i, p, 2 * MI + 2 * i + p)
            unit(0, True, 2)
            with dve.Fori(1, NU - 2) as u:
                unit(u, False, 2)
            unit(NU - 2, False, 1)

            def halves(c, ft, bank):
                i = KT * c + ft
                dve.wait_ge(tr_ps, KT * ln(1, c) + ft + 1)
                if i == 0:
                    dve.wait_ge(wg_s, 2 * KT)
                if i >= 2:
                    dve.wait_ge(h_lo_s, i - 1)
                scale, shift = mcol[0][:, 8 + ft:9 + ft], mcol[0][:, 6 + ft:7 + ft]
                nc.vector.tensor_scalar(hT_hi[:, ft, CH * c:CH * (c + 1)], ps[:, bank, :], scale, shift,
                                        ALU.mult, ALU.add).then_inc(h_hi_s, 1)
                nc.vector.tensor_scalar(h32[ft][:], ps[:, bank, :], scale, shift, ALU.mult, ALU.add).then_inc(h_full_s, 1)

            rt_n = [0]

            def rt_then(ins):
                rt_n[0] += 1
                ins.then_inc(rt, 1)
                dve.wait_ge(rt, rt_n[0])

            def router(c, bank, col):
                all_e = [P, TPC, E]
                logit = ps[:, bank, col:col + TPC * E].rearrange("p (t e) -> p t e", e=E)
                dve.wait_ge(lg_ps, c + 1)
                rt_then(nc.vector.tensor_reduce(r4[:], logit, AX.X, ALU.max))
                rt_then(nc.vector.tensor_copy(ce[:], logit))
                nc.vector.tensor_tensor(lg[:], ce[:], r4[:].unsqueeze(2).to_broadcast(all_e), ALU.subtract).then_inc(lg_s, 1)
                dve.wait_ge(exp_s, c + 1)
                rt_then(nc.vector.tensor_reduce(r4[:], pr[:], AX.X, ALU.add))
                rt_then(nc.vector.reciprocal(r4b[:], r4[:]))
                rt_then(nc.vector.tensor_tensor(pr[:], pr[:], r4b[:].unsqueeze(2).to_broadcast(all_e), ALU.mult))
                other = pr[:].unsqueeze(2).to_broadcast([P, TPC, E, E])
                own = pr[:].unsqueeze(3).to_broadcast([P, TPC, E, E])
                nc.vector.tensor_tensor(cmp1[:], other, own, ALU.is_gt)
                rt_then(nc.vector.tensor_tensor(cmp2[:], other, own, ALU.is_equal))
                dve.wait_ge(sel_s, 1)
                rt_then(nc.vector.tensor_tensor(cmp2[:], cmp2[:], tri[:].unsqueeze(1).to_broadcast([P, TPC, E, E]), ALU.mult))
                rt_then(nc.vector.tensor_tensor(cmp1[:], cmp1[:], cmp2[:], ALU.add))
                rt_then(nc.vector.tensor_reduce(rank[:], cmp1[:], AX.X, ALU.add))
                rt_then(nc.vector.scalar_tensor_tensor(ce[:], rank[:], 2.0, pr[:], ALU.is_lt, ALU.mult))
                rt_then(nc.vector.tensor_reduce(r4[:], ce[:], AX.X, ALU.add))
                rt_then(nc.vector.reciprocal(r4b[:], r4[:]))
                rt_then(nc.vector.tensor_tensor(ce[:], ce[:], r4b[:].unsqueeze(2).to_broadcast(all_e), ALU.mult))
                if c:
                    dve.wait_ge(ce_ps, c)
                rt_then(nc.vector.tensor_copy(ce3[:, :, 0, 0:E], ce[:]))
                rt_then(nc.vector.tensor_tensor(ce[:], ce[:], ce3[:, :, 0, 0:E], ALU.subtract))
                rt_then(nc.vector.tensor_copy(ce3[:, :, 1, 0:E], ce[:]))
                nc.vector.tensor_tensor(ce3[:, :, 2, 0:E], ce[:], ce3[:, :, 1, 0:E], ALU.subtract).then_inc(ce_s, 1)

            def combine_rows(c, bank):
                dve.wait_ge(ce_ps, c + 1)
                nc.vector.tensor_copy(ceT[:, CH * c:CH * (c + 1)], ps[0:3 * CR, bank, :]).then_inc(ceT_s, 1)

            dve.wait_ge(qd_out, 16 * KT * NC)
            dve.wait_ge(att_s, NG * (NC - 1))
            statistics(1, 0)
            normalise(1, 0)
            statistics(1, 1)
            for ft in range(KT):
                halves(0, ft, 1 + ft)
            normalise(1, 1)
            statistics(1, 2)
            router(0, 3, 0)
            invert_sums(NU - 2)
            for ft in range(KT):
                halves(1, ft, 1 + ft)
            combine_rows(0, 0)
            normalise(1, 2)
            router(1, 3, 32)
            for ft in range(KT):
                halves(2, ft, 1 + ft)
            combine_rows(1, 0)
            router(2, 3, 64)
            combine_rows(2, 0)
            early, late = slice(0, P * EARLY), slice(P * EARLY, IA)
            dve.wait_ge(wu_hi_s, 1)
            nc.vector.tensor_tensor(wu_lo[:, :, early], wu_raw[:, :, early], wu_hi[:, :, early].bitcast(F32),
                                    ALU.subtract).then_inc(wu_s, 1)
            invert_sums(NU - 1)
            dve.wait_ge(wu_hi_s, 2)
            nc.vector.tensor_tensor(wu_lo[:, :, late], wu_raw[:, :, late], wu_hi[:, :, late].bitcast(F32),
                                    ALU.subtract).then_inc(wu_s, 1)
            dve.wait_ge(wd_hi_s, 1)
            nc.vector.tensor_tensor(wd_lo[:, 0:EARLY, :], wd_raw[:, 0:EARLY, :], wd_hi[:, 0:EARLY, :].bitcast(F32),
                                    ALU.subtract).then_inc(wd_s, 1)

            def chunk(c, slots, first=False):
                for it in range(NI):
                    rows = P if it < NI - 1 else LAST
                    n = c * NI + it
                    dve.wait_ge(sig_s, n + 1)
                    dve.wait_ge(u_ps, n + 1)
                    if not (first and it < 2):
                        dve.wait_ge(hid_lo_s, n - 1)
                    if it == 1 and not first:
                        dve.wait_ge(y_s, c)
                    full = hid[0:rows, it % 2, :]
                    nc.vector.scalar_tensor_tensor(full, ps[0:rows, 2 + it % 2, :], bu[0:rows, it:it + 1],
                                                   sig[0:rows, it % 2, :], ALU.add, ALU.mult).then_inc(t_s, 1)
                    dve.wait_ge(t_s, n + 1)
                    if it < IE:
                        dve.wait_ge(cb_ps, c * IE + it + 1)
                        nc.vector.tensor_tensor(full, ps[:, 4, :], full, ALU.mult).then_inc(full_s, 1)
                    dve.wait_ge(hid_hi_s, n + 1)
                    nc.vector.tensor_tensor(hid_lo[0:rows, it % 2, :], full, hid_hi[0:rows, it % 2, :].bitcast(F32),
                                            ALU.subtract).then_inc(hid_lo_s, 1)
                    for work in slots.get(it, ()):
                        work(c)

            def gate_sums(c, c_lo):
                dve.wait_ge(hid_used, (c + 1) * NI)
                dve.wait_ge(hid_lo_s, c_lo)
                gb = rows0[:, GB, :].unsqueeze(1).to_broadcast([P, TPC, D])
                yt = hid[:].rearrange("p b (j d) -> p (b j) d", j=2)
                nc.vector.tensor_tensor(yt, ps[:, 6:8, :].rearrange("p b (j d) -> p (b j) d", j=2), gb,
                                        ALU.mult).then_inc(y_read, 1)
                dve.wait_ge(y_read, c + 1)
                dve.wait_ge(xsd_s, c + 1)
                nc.vector.tensor_tensor(x_cols(c * TPC, TPC), x_cols(c * TPC, TPC), hid[:].rearrange("p b n -> p (b n)"),
                                        ALU.add).then_inc(y_s, 1)

            def row1(j):
                def work(c):
                    dve.wait_ge(row_ps, j + 1)
                    nc.vector.tensor_copy(mrow1[:, 2 * j:2 * j + 2, :].rearrange("p a d -> p (a d)"),
                                          ps[:, 5, :]).then_inc(row_s, 1)
                return work

            def rows_of_l1(c):
                dve.wait_ge(row_s, 3)
                then(modulation_rows(mrow1, rows1))
                dve.wait_ge(l1_in, 48)
                nc.vector.tensor_tensor(gsd[:], sdb_row[:], rows0[:, GB, :], ALU.mult)
                nc.vector.tensor_tensor(gb1[:], b1_row[:], rows1[:, GB, :], ALU.mult).then_inc(gb1_s, 1)
                nc.vector.tensor_scalar(rows1[:, RGA, :], rows1[:, GA, :], r_col[:, 0:1], None, ALU.mult).then_inc(rows1_s, 1)

            def complete3(c):
                dve.wait_ge(att_s, NU)
                statistics(1, NC - 1)

            chunk(0, {2: [lambda c: (dve.wait_ge(att_s, NU), broadcast_c(1, cb1))], 3: [complete3],
                      4: [lambda c: normalise(1, NC - 1)],
                      5: [lambda c: halves(NC - 1, 0, 5)], 6: [lambda c: halves(NC - 1, 1, 5)],
                      7: [lambda c: router(NC - 1, 5, 0)], 8: [lambda c: combine_rows(NC - 1, 5)],
                      9: [lambda c: columns(1, 5)], 10: [row1(0)], 11: [row1(1)], 12: [row1(2)], 13: [rows_of_l1]},
                  first=True)

            def l1_begin(c):
                gate_sums(c - 1, c * NI if isinstance(c, int) and c == NC else c * NI + 1)
                statistics(2, c - 1, (y_s, c))

            def first_tokens(c):
                dve.wait_ge(xh_s, TPC * (ln(2, 0) + 1))
                then(nc.vector.scalar_tensor_tensor(ux[:], mrow1[0:DX, 1, :], 1.0, xh1[0:DX, 0, :], ALU.add, ALU.mult))
                nc.vector.tensor_tensor(ux[:], ux[:], mrow1[0:DX, 0, :], ALU.add).then_inc(ux_s, 1)

            def leave_uw(c):
                dve.wait_ge(uw_ps, 1)
                nc.vector.tensor_copy(uu[:], ps[0:DX, 5, 0:D])
                nc.vector.tensor_copy(ww[:], ps[0:DX, 5, D:2 * D]).then_inc(uw_s, 1)

            def add_product(c, half, ready, read, done, row):
                d = c - 1
                dve.wait_ge(ready, 2 * d + half + 1)
                nc.vector.tensor_tensor(yt2[:], ps[:, 5, :].rearrange("p (j d) -> p j d", j=2),
                                        rows1[:, row, :].unsqueeze(1).to_broadcast([P, 2, D]), ALU.mult).then_inc(read, 1)
                dve.wait_ge(read, 2 * d + half + 1)
                xs = x_cols(d * TPC + 2 * half, 2)
                nc.vector.tensor_tensor(xs, xs, yt2[:].rearrange("p j d -> p (j d)"), ALU.add).then_inc(done, 1)

            def attend(half):
                def work(c):
                    dve.wait_ge(res1_s, c)
                    if half:
                        dve.wait_ge(za_s, 2 * c - 1)
                    else:
                        dve.wait_ge(f_s, 2 * (c - 1))
                    add_product(c, half, za_ps, za_read, za_s, RGA)
                return work

            def attend_first(c):
                dve.wait_ge(res1_s, 1)
                dve.wait_ge(za_ps, 1)
                dve.wait_ge(gb1_s, 1)
                b = ps[:, 5, :].rearrange("p (j d) -> p j d", j=2)
                nc.vector.tensor_copy(xa[:], b[0:DX, 0, :]).then_inc(xa_s, 1)
                nc.vector.tensor_tensor(yt2[32:64, 0, :], b[32:64, 0, :], rows1[32:64, RGA, :], ALU.mult)
                nc.vector.tensor_tensor(yt2[64:128, 0, :], b[64:128, 0, :], rows1[64:128, RGA, :], ALU.mult)
                nc.vector.tensor_tensor(yt2[:, 1, :], b[:, 1, :], rows1[:, RGA, :], ALU.mult).then_inc(za_read, 1)

            def attend_a(c):
                dve.wait_ge(axa_ps, 1)
                nc.vector.tensor_tensor(yt2[0:DX, 0, :], ps[0:DX, 5, 0:D], rows1[0:DX, GA, :], ALU.mult).then_inc(axa_s, 1)
                dve.wait_ge(axa_s, 1)
                dve.wait_ge(za_read, 1)
                nc.vector.tensor_tensor(x_cols(0, 2), x_cols(0, 2), yt2[:].rearrange("p j d -> p (j d)"), ALU.add).then_inc(za_s, 1)
                dve.wait_ge(za_s, 1)

            def binarise(c):
                then(nc.vector.tensor_reduce(alpha[:], w1_sb[:], AX.X, ALU.add, apply_absolute_value=True))
                then(nc.vector.tensor_scalar(alpha[:], alpha[:], 1.0 / D, None, ALU.mult))
                then(nc.vector.tensor_scalar(bw[:], w1_sb[:], 0.0, 2.0, ALU.is_ge, ALU.mult))
                for k in range(KT):
                    ins = nc.vector.tensor_scalar(bw[:, k, :], bw[:, k, :], -1.0, alpha[:, k:k + 1], ALU.add, ALU.mult)
                then(ins)
                then(nc.vector.tensor_tensor(bw[:], bw[:], w1_sb[:], ALU.subtract))
                nc.vector.tensor_tensor(bw[:], bw[:], w1_sb[:], ALU.add).then_inc(bw_s, 1)

            def leave_bw(c):
                dve.wait_ge(bwT_ps, 1)
                nc.vector.tensor_copy(bwT[:].rearrange("p k o -> p (k o)"), ps[:, 5, :]).then_inc(bwT_s, 1)

            def feed(half):
                def work(c):
                    dve.wait_ge(xb_s, c)
                    if half:
                        dve.wait_ge(f_s, 2 * c - 1)
                    else:
                        dve.wait_ge(za_s, 2 * c)
                    add_product(c, half, f_ps, f_read, f_s, GB)
                return work

            second = [attend(1), lambda c: statistics(3, c - 1, (za_s, 2 * c))]
            rest = {0: [l1_begin], 1: [lambda c: normalise(2, c - 1)], 6: [attend(0)], 8: second,
                    9: [lambda c: normalise(3, c - 1)], 12: [feed(0)], 13: [feed(1)]}
            chunk(1, {**rest, 1: rest[1] + [first_tokens], 3: [binarise], 4: [leave_uw], 6: [attend_first], 7: [attend_a],
                      9: rest[9] + [leave_bw]})
            with dve.Fori(2, NC) as c:
                chunk(c, rest)
            for it in sorted(rest):
                for work in rest[it]:
                    work(NC)

        @block.gpsimd
        def _(pool):
            setup = [0]

            def then(ins):
                setup[0] += 1
                ins.then_inc(res_step, 1)
                pool.wait_ge(res_step, setup[0])

            then(nc.gpsimd.memset(m05[:], -0.5))
            then(nc.gpsimd.memset(ident[:], 0.0))
            nc.gpsimd.affine_select(ident[:], ident[:], [[-1, P]], ALU.not_equal, 1.0, base=0,
                                    channel_multiplier=1).then_inc(consts, 1)
            pool.wait_ge(consts, 1)
            one_pair = struct.unpack("<f", struct.pack("<I", 0x3F803F80))[0]
            nc.gpsimd.memset(kst[KR:KR + NM].rearrange("p h t -> p (h t)").bitcast(F32), one_pair).then_inc(kst_one, 1)
            pool.wait_ge(kst_one, 1)

            def deviation(n, c):
                q = ln(n, c)
                cols = slice(TPC * c, TPC * (c + 1)) if n == 0 else slice(0, TPC)
                mv, rs = (mv0, rs0) if n == 0 else (mv1, rs1)
                pool.wait_ge(var_s, TPC * (q + 1))
                nc.gpsimd.tensor_scalar(veps[:], mv[:, cols, 1], EPS, None, ALU.add).then_inc(veps_s, 1)
                pool.wait_ge(veps_s, q + 1)
                nc.gpsimd.tensor_tensor(rs[:, cols], veps[:], m05[:], ALU.pow).then_inc(rs_s, 1)
                pool.wait_ge(rs_s, q + 1)

            for c in range(NC):
                deviation(0, c)
            pool.wait_ge(proj_ps, 2 * KT * NC)
            pool.wait_ge(mrow_ready, 1)
            nc.gpsimd.memset(vp[:, :, :, DH + 1:VW], 0.0)
            nc.gpsimd.memset(vp[:, :, :, DH], 1.0).then_inc(vconst, 1)
            pool.wait_ge(vconst, 1)

            def split_max(v):
                pool.wait_ge(nmT_s, v + 1)
                pool.wait_ge(nm_in, v * (16 * NM))
                nc.gpsimd.tensor_copy(nmp[:, 0, :], nm32[:]).then_inc(nm_step, 1)
                pool.wait_ge(nm_step, v * 3 + 1)
                nc.gpsimd.tensor_tensor(nmr[:], nm32[:], nmp[:, 0, :], ALU.subtract).then_inc(nm_step, 1)
                pool.wait_ge(nm_step, v * 3 + 2)
                nc.gpsimd.tensor_copy(nmp[:, 1, :], nmr[:]).then_inc(nm_step, 1)
                pool.wait_ge(nm_step, v * 3 + 3)
                nc.gpsimd.tensor_tensor(nmp[:, 2, :], nmr[:], nmp[:, 1, :], ALU.subtract).then_inc(nm_s, 1)

            def residual(lo, hi):
                for t in range(lo, hi):
                    then(nc.gpsimd.tensor_scalar(xt[:], x[:, t, :], mv0[:, t, 0:1], rs0[:, t:t + 1],
                                                 ALU.subtract, ALU.mult))
                    then(nc.gpsimd.tensor_tensor(xt[:], xt[:], rows0[:, GCA, :], ALU.mult))
                    then(nc.gpsimd.tensor_tensor(xt[:], xt[:], rows0[:, GSA, :], ALU.add))
                    then(nc.gpsimd.tensor_tensor(x[:, t, :], x[:, t, :], xt[:], ALU.add))

            def add_attention(u, c, g):
                pool.wait_ge(rec_s, u + 1)
                nc.gpsimd.tensor_tensor(att_u[:], o_tm[:, :, :, 0:DH], rec[:].unsqueeze(3).to_broadcast([P, TPC, G, DH]),
                                        ALU.mult).then_inc(att_step, 1)
                pool.wait_ge(att_step, u * 2 + 1)
                w = G * DH
                flat = att_u[:].rearrange("p j k d -> p j (k d)")
                nc.gpsimd.tensor_tensor(flat, flat, rows0[:, GA, w * g:w * (g + 1)].unsqueeze(1).to_broadcast([P, TPC, w]),
                                        ALU.mult).then_inc(att_step, 1)
                pool.wait_ge(att_step, u * 2 + 2)
                dst = x[:, c * TPC:(c + 1) * TPC, w * g:w * (g + 1)]
                nc.gpsimd.tensor_tensor(dst, dst, flat, ALU.add).then_inc(att_s, 1)

            split_max(0)
            pool.wait_ge(nm_s, 1)
            pool.wait_ge(split_s, KT * NC)
            pool.wait_ge(kd_out, 16 * KT * NC)
            residual(0, NT // 2)
            split_max(1)
            pool.wait_ge(nm_s, 2)
            residual(NT // 2, NT)

            def router_constants():
                then(nc.gpsimd.memset(sel[:], 1.0))
                for a in range(3):
                    s_a = sel[CR * a:CR * (a + 1), :]
                    then(nc.gpsimd.affine_select(s_a, s_a, [[1, E * I]], ALU.is_ge, 0.0, base=0, channel_multiplier=-I))
                    then(nc.gpsimd.affine_select(s_a, s_a, [[-1, E * I]], ALU.is_ge, 0.0, base=I - 1, channel_multiplier=I))
                nc.gpsimd.tensor_copy(rw_hi[:], rw[:]).then_inc(rw_s, 1)
                pool.wait_ge(rw_s, 1)
                nc.gpsimd.tensor_tensor(rw_lo[:], rw[:], rw_hi[:].bitcast(F32), ALU.subtract).then_inc(rw_s, 1)

            def router_tables():
                then(nc.gpsimd.memset(ce3[:], 0.0))
                then(nc.gpsimd.tensor_copy(ident_bf[:], ident[:]))
                then(nc.gpsimd.memset(tri[:], 1.0))
                nc.gpsimd.affine_select(tri[:], tri[:], [[1, E], [-1, E]], ALU.is_gt, 0.0, base=0,
                                        channel_multiplier=0).then_inc(sel_s, 1)
                pool.wait_ge(sel_s, 1)

            def gate_rounded():
                pool.wait_ge(ffw_in[0], 48)
                for k in range(KT):
                    nc.gpsimd.tensor_copy(wg_hi[:, k, :], wg_raw[:, k, :]).then_inc(wg_s, 1)

            def gate_rest():
                pool.wait_ge(wg_s, KT)
                for k in range(KT):
                    nc.gpsimd.tensor_tensor(wg_lo[:, k, :], wg_raw[:, k, :], wg_hi[:, k, :].bitcast(F32),
                                            ALU.subtract).then_inc(wg_s, 1)

            def input_rest(c):
                for ft in range(KT):
                    i = KT * c + ft
                    pool.wait_ge(h_full_s, i + 1)
                    nc.gpsimd.tensor_tensor(hT_lo[:, CH * i:CH * (i + 1)], h32[ft][:],
                                            hT_hi[:, ft, CH * c:CH * (c + 1)].bitcast(F32), ALU.subtract).then_inc(h_lo_s, 1)

            for u in range(NU - 1):
                if u == NU - 2:
                    deviation(1, 0)
                    deviation(1, 1)
                    input_rest(0)
                    deviation(1, 2)
                add_attention(u, u // NG, u % NG)
                pool.wait_ge(att_s, u + 1)
                if u == 4:
                    gate_rounded()
                if u == 6:
                    router_constants()
                if u == NU - NG:
                    pool.wait_ge(sc_ps, G * MT * (NU - NG + 1))
                    gate_rest()
                    router_tables()
                if u + 2 < NU:
                    split_max(u + 2)
                    pool.wait_ge(nm_s, u + 3)
            input_rest(1)
            input_rest(2)
            add_attention(NU - 1, NC - 1, NG - 1)
            pool.wait_ge(att_s, NU)
            pool.wait_ge(pv_s, MT * NU)
            pool.wait_ge(ffw_in[2], 48)
            pieces = [(slice(0, P), slice(EARLY, NI - 1)), (slice(0, LAST), slice(NI - 1, NI))]
            for rows, tiles in pieces:
                nc.gpsimd.tensor_copy(wd_hi[rows, tiles, :], wd_raw[rows, tiles, :]).then_inc(wd2_s, 1)
            pool.wait_ge(wd2_s, 2)
            for rows, tiles in pieces:
                nc.gpsimd.tensor_tensor(wd_lo[rows, tiles, :], wd_raw[rows, tiles, :], wd_hi[rows, tiles, :].bitcast(F32),
                                        ALU.subtract).then_inc(wd2_s, 1)
            deviation(1, NC - 1)
            pool.wait_ge(sc_ps, G * MT * NU)
            input_rest(NC - 1)
            pool.wait_ge(gb1_s, 1)
            for c in range(NC):
                xs = x[:, TPC * c:TPC * (c + 1), :]
                nc.gpsimd.tensor_tensor(xs, xs, gsd[:].unsqueeze(1).to_broadcast([P, TPC, D]), ALU.add).then_inc(xsd_s, 1)
            pool.wait_ge(rows1_s, 1)
            for d in range(NC):
                deviation(2, d)
                pool.wait_ge(y_s, d + 1)
                pool.wait_ge(xh_s, TPC * (ln(2, d) + 1))
                for j in range(TPC):
                    t = TPC * d + j
                    nc.gpsimd.tensor_tensor(xt1[:], xh1[:, j, :], rows1[:, GCA, :], ALU.mult).then_inc(res1_step, 1)
                    pool.wait_ge(res1_step, 3 * t - d + 1)
                    nc.gpsimd.tensor_tensor(xt1[:], xt1[:], rows1[:, GSA, :], ALU.add).then_inc(res1_step, 1)
                    pool.wait_ge(res1_step, 3 * t - d + 2)
                    ins = nc.gpsimd.tensor_tensor(x[:, t, :], x[:, t, :], xt1[:], ALU.add)
                    if j < TPC - 1:
                        ins.then_inc(res1_step, 1)
                        pool.wait_ge(res1_step, 3 * t - d + 3)
                    else:
                        ins.then_inc(res1_s, 1)
                        pool.wait_ge(res1_s, d + 1)
                if d == 0:
                    pool.wait_ge(relu_s, 1)
                    nc.gpsimd.affine_select(att[:, KT - 1, :], att[:, KT - 1, :], [[1, D]], ALU.not_equal, 0.0,
                                            base=-((P - 1) * D + D - 1), channel_multiplier=D).then_inc(att_z, 1)
                deviation(3, d)
                pool.wait_ge(xh_s, TPC * (ln(3, d) + 1))
                xs = x[:, TPC * d:TPC * (d + 1), :]
                nc.gpsimd.tensor_tensor(xs, xs, gb1[:].unsqueeze(1).to_broadcast([P, TPC, D]), ALU.add).then_inc(xb_s, 1)

    return nc


def kernel(L0_attn_x, L0_attn_Wq, L0_attn_bq, L0_attn_Wk, L0_attn_bk, L0_attn_Wv, L0_attn_bv, L0_ffn_router_w,
           L0_ffn_gate_w, L0_ffn_up_w, L0_ffn_down_w, L0_ffn_s_gate_w, L0_ffn_s_gate_b, L0_ffn_s_up_w,
           L0_ffn_s_up_b, L0_ffn_s_down_w, L0_ffn_s_down_b, L0_c, L0_wmod, L1_attn_A_l, L1_attn_r_l, L1_attn_B_l,
           L1_attn_C_l, L1_ffn_weight, L1_ffn_bias, L1_c, L1_wmod):
    import concourse.bacc as bacc
    from concourse.bass_utils import run_bass_kernel_spmd

    laid = [("x", np.asarray(L0_attn_x).reshape(T, D)),
            ("wq", L0_attn_Wq), ("bq", L0_attn_bq), ("wk", L0_attn_Wk), ("bk", L0_attn_bk), ("wv", L0_attn_Wv),
            ("bv", L0_attn_bv), ("routerT", np.asarray(L0_ffn_router_w).T), ("gate_w", L0_ffn_gate_w),
            ("up_w", L0_ffn_up_w), ("down_w", L0_ffn_down_w), ("sg_w", L0_ffn_s_gate_w), ("sg_b", L0_ffn_s_gate_b),
            ("su_w", L0_ffn_s_up_w), ("su_b", L0_ffn_s_up_b), ("sd_w", L0_ffn_s_down_w), ("sd_b", L0_ffn_s_down_b),
            ("c0", L0_c), ("wmod0", L0_wmod), ("AT", np.asarray(L1_attn_A_l).T), ("r_l", L1_attn_r_l),
            ("BT", np.asarray(L1_attn_B_l).T), ("CT", np.asarray(L1_attn_C_l).T), ("w1", L1_ffn_weight),
            ("b1", L1_ffn_bias), ("c1", L1_c), ("wmod1", L1_wmod)]
    nc = bacc.Bacc("TRN2", target_bir_lowering=False, num_devices=1)
    arrays, args = {}, []
    for name, a in laid:
        arrays[name] = np.ascontiguousarray(a)
        args.append(nc.dram_tensor(name, arrays[name].shape, F32, kind="ExternalInput").ap())
    args.append(nc.dram_tensor("out", (T, D), F32, kind="ExternalOutput").ap())
    build(nc, *args)
    got = run_bass_kernel_spmd(nc, [arrays], core_ids=[0]).results[0]["out"]
    return got.reshape(1, T, D)
```
